# Optimizing a Trainium2 kernel written in Bass

```python
import numpy as np
import jax
import jax.numpy as jnp

def _softmax(x, axis=-1):
    return jax.nn.softmax(x, axis=axis)

def _gelu(x):
    return jax.nn.gelu(x, approximate=True)

def _silu(x):
    return jax.nn.silu(x)

def _sigmoid(x):
    return jax.nn.sigmoid(x)

def _layernorm(x, axis=-1, eps=1e-05):
    m = jnp.mean(x, axis=axis, keepdims=True)
    v = jnp.var(x, axis=axis, keepdims=True)
    return (x - m) / jnp.sqrt(v + eps)

def _scatter_add(tgt, idx, src, axis=0):
    return tgt.at[idx].add(src)

def _segment_sum(src, seg, n):
    return jax.ops.segment_sum(src, seg, n)
kernel_name = 'mk_adaln_attn_ffn_d1_seqx_r8_5d1dbd'

def setup_inputs(seed: int=0):
    np.random.seed(seed)
    _w = jnp.asarray

    def _rec_inputs():
        import jax
        import jax.numpy as jnp
        _rk = jax.random.key(seed)
        x = -7.109e-05 + 0.9999 * jax.random.normal(jax.random.fold_in(_rk, 1), (64, 32, 512), jnp.float32)
        _lenS = 32 - jax.random.randint(jax.random.fold_in(_rk, 7), (64,), 0, max(1, 32 // 4) + 1, jnp.int32)
        _lenS2 = 32 - jax.random.randint(jax.random.fold_in(_rk, 8), (64,), 0, max(1, 32 // 4) + 1, jnp.int32)
        itok_B_0_15 = jax.random.randint(jax.random.fold_in(_rk, 11), (64,), 0, 16, jnp.int32)
        itok_B_9_3973 = jax.random.randint(jax.random.fold_in(_rk, 12), (64,), 9, 3974, jnp.int32)
        return (x, itok_B_0_15, itok_B_9_3973)
    x, itok_B_0_15, itok_B_9_3973 = _rec_inputs()

    def _L0_cond_setup():
        import jax, jax.numpy as jnp
        import numpy as np
        NUM_CONDITIONS = 16
        IN_CH = 32
        OUT_CH = 32
        B = 64
        T = 512
        key = jax.random.key(seed)
        k_x, k_w, k_c = jax.random.split(key, 3)
        x = jax.random.normal(k_x, (B, IN_CH, T), dtype=jnp.float32)
        bound = float(np.sqrt(6.0 / IN_CH))
        weights = jax.random.uniform(k_w, (NUM_CONDITIONS, IN_CH, OUT_CH), dtype=jnp.float32, minval=-bound, maxval=bound)
        condition = jax.random.randint(k_c, (B,), 0, NUM_CONDITIONS, dtype=jnp.int64)
        return {'x': x, 'weights': weights, 'condition': condition}
    _L0_cond_all = _L0_cond_setup()
    _L0_cond_in = {k: v for k, v in _L0_cond_all.items() if k in ('weights',)}
    del _L0_cond_all

    def _L0_attn_setup():
        import jax, jax.numpy as jnp
        import numpy as np
        H = 512
        D = H // 4
        key = jax.random.key(seed)
        k1, k2, k3, k4, k5 = jax.random.split(key, 5)
        x = jax.random.normal(k1, (4, 512, H), dtype=jnp.float32)
        s_in = 1.0 / np.sqrt(H)
        Wqkv = jax.random.normal(k2, (H, 3 * D), dtype=jnp.float32) * s_in
        bqkv = jax.random.normal(k3, (3 * D,), dtype=jnp.float32) * 0.01
        Wo = jax.random.normal(k4, (D, H), dtype=jnp.float32) * (1.0 / np.sqrt(D))
        bo = jax.random.normal(k5, (H,), dtype=jnp.float32) * 0.01
        return {'x': x, 'Wqkv': Wqkv, 'bqkv': bqkv, 'Wo': Wo, 'bo': bo}
    _L0_attn_all = _L0_attn_setup()
    _L0_attn_in = {k: v for k, v in _L0_attn_all.items() if k in ('Wqkv', 'bqkv', 'Wo', 'bo')}
    del _L0_attn_all

    def _L0_cond2_setup():
        import jax, jax.numpy as jnp
        import numpy as np
        from jax import lax
        B, E, T = (32, 64, 512)
        K = 5
        PAD = (K - 1) // 2
        key = jax.random.key(seed)
        k1, k2, k3 = jax.random.split(key, 3)
        x = jax.random.normal(k1, (B, E, T), dtype=jnp.float32)
        length = jax.random.randint(k2, (B,), 1, T + 1, dtype=jnp.int64)
        conv_w = jax.random.normal(k3, (1, 1, K), dtype=jnp.float32) * (1.0 / np.sqrt(K))
        return {'x': x, 'length': length, 'conv_w': conv_w}
    _L0_cond2_all = _L0_cond2_setup()
    _L0_cond2_in = {k: v for k, v in _L0_cond2_all.items() if k in ('conv_w',)}
    del _L0_cond2_all

    def _L0_ffn_setup():
        import jax, jax.numpy as jnp
        import numpy as np
        BLOCK = 32
        E4M3_MAX = 448.0
        EMAX_E4M3 = 8

        def quantize_mx(x2d):
            M, K = x2d.shape
            xb = x2d.reshape(M, K // BLOCK, BLOCK)
            amax = jnp.max(jnp.abs(xb), axis=-1)
            exp = jnp.floor(jnp.log2(jnp.maximum(amax, 1e-38))) - EMAX_E4M3
            exp = jnp.clip(exp, -127.0, 127.0)
            scale = jnp.exp2(exp)
            q = jnp.clip(xb / scale[..., None], -E4M3_MAX, E4M3_MAX)
            q = q.astype(jnp.float8_e4m3fn)
            return (q, scale)

        def dequant(q, scale):
            M, G, B = q.shape
            return (q.astype(jnp.float32) * scale[..., None]).reshape(M, G * B)
        key = jax.random.key(seed)
        k1, k2, k3 = jax.random.split(key, 3)
        B, S, K, N = (4, 256, 512, 512)
        x = jax.random.normal(k1, (B, S, K), dtype=jnp.float32)
        weight = jax.random.normal(k2, (N, K), dtype=jnp.float32) * 0.02
        bias = jax.random.normal(k3, (N,), dtype=jnp.float32) * 0.02
        return {'x': x, 'weight': weight, 'bias': bias}
    _L0_ffn_all = _L0_ffn_setup()
    _L0_ffn_in = {k: v for k, v in _L0_ffn_all.items() if k in ('weight', 'bias')}
    del _L0_ffn_all
    return {'x': x, 'itok_B_0_15': itok_B_0_15, 'itok_B_9_3973': itok_B_9_3973, 'L0_cond_weights': _L0_cond_in['weights'], 'L0_attn_Wqkv': _L0_attn_in['Wqkv'], 'L0_attn_bqkv': _L0_attn_in['bqkv'], 'L0_attn_Wo': _L0_attn_in['Wo'], 'L0_attn_bo': _L0_attn_in['bo'], 'L0_cond2_conv_w': _L0_cond2_in['conv_w'], 'L0_ffn_weight': _L0_ffn_in['weight'], 'L0_ffn_bias': _L0_ffn_in['bias']}

def reference(x, itok_B_0_15, itok_B_9_3973, L0_cond_weights, L0_attn_Wqkv, L0_attn_bqkv, L0_attn_Wo, L0_attn_bo, L0_cond2_conv_w, L0_ffn_weight, L0_ffn_bias):
    import jax
    import jax.numpy as jnp

    def _L0_cond_ref(x, weights, condition):
        import jax, jax.numpy as jnp
        import numpy as np
        NUM_CONDITIONS = 16
        IN_CH = 32
        OUT_CH = 32
        B = 64
        T = 512
        W = weights[condition]
        return jnp.einsum('bct,bcd->bdt', x, W)

    def _L0_attn_ref(x, Wqkv, bqkv, Wo, bo):
        import jax, jax.numpy as jnp
        import numpy as np
        H = 512
        D = H // 4
        B, S, C = x.shape
        d = C // 4
        qkv = jnp.einsum('bsc,cf->bsf', x, Wqkv) + bqkv
        qkv = qkv.reshape(B, S, 3, d)
        q, k, v = (qkv[:, :, 0], qkv[:, :, 1], qkv[:, :, 2])
        scale = 1.0 / jnp.sqrt(jnp.float32(d)).astype(x.dtype)
        attn = jnp.einsum('bqd,bkd->bqk', q, k) * scale
        attn = jax.nn.softmax(attn, axis=-1)
        out = jnp.einsum('bqk,bkd->bqd', attn, v)
        return jnp.einsum('bqd,dc->bqc', out, Wo) + bo

    def _L0_cond2_ref(x, length, conv_w):
        import jax, jax.numpy as jnp
        import numpy as np
        from jax import lax
        B, E, T = (32, 64, 512)
        K = 5
        PAD = (K - 1) // 2
        mask = (jnp.arange(T)[None, :] < length[:, None]).astype(x.dtype)
        denom = length.astype(x.dtype)[:, None]
        y = jnp.einsum('bet,bt->be', x, mask) / denom
        yc = lax.conv_general_dilated(y[:, None, :], conv_w, window_strides=(1,), padding=[(PAD, PAD)], dimension_numbers=('NCH', 'OIH', 'NCH'))[:, 0, :]
        gate = jax.nn.sigmoid(yc)
        return x * gate[:, :, None]

    def _L0_ffn_ref(x, weight, bias):
        import jax, jax.numpy as jnp
        import numpy as np
        BLOCK = 32
        E4M3_MAX = 448.0
        EMAX_E4M3 = 8

        def quantize_mx(x2d):
            M, K = x2d.shape
            xb = x2d.reshape(M, K // BLOCK, BLOCK)
            amax = jnp.max(jnp.abs(xb), axis=-1)
            exp = jnp.floor(jnp.log2(jnp.maximum(amax, 1e-38))) - EMAX_E4M3
            exp = jnp.clip(exp, -127.0, 127.0)
            scale = jnp.exp2(exp)
            q = jnp.clip(xb / scale[..., None], -E4M3_MAX, E4M3_MAX)
            q = q.astype(jnp.float8_e4m3fn)
            return (q, scale)

        def dequant(q, scale):
            M, G, B = q.shape
            return (q.astype(jnp.float32) * scale[..., None]).reshape(M, G * B)
        lead = x.shape[:-1]
        K = x.shape[-1]
        x2 = x.reshape(-1, K)
        xq, xs = quantize_mx(x2)
        wq, ws = quantize_mx(weight)
        out = dequant(xq, xs) @ dequant(wq, ws).T + bias
        out = out.astype(jnp.bfloat16)
        return out.reshape(*lead, out.shape[-1])
    x = x + _L0_attn_ref(_L0_cond_ref(x, L0_cond_weights, itok_B_0_15), L0_attn_Wqkv, L0_attn_bqkv, L0_attn_Wo, L0_attn_bo)
    x = x + _L0_ffn_ref(_L0_cond2_ref(x, itok_B_9_3973, L0_cond2_conv_w), L0_ffn_weight, L0_ffn_bias)
    return x

_drawn_inputs = setup_inputs


def setup_inputs(seed=0):
    import zlib

    import numpy as np

    out = dict(_drawn_inputs(seed))
    spreads = {}
    factors = {'L0_attn_bqkv': 5.092, 'L0_attn_bo': 6.511, 'L0_cond2_conv_w': 7.417, 'L0_ffn_bias': 3.625}
    for name, (base, spread) in spreads.items():
        noise = np.random.default_rng([zlib.crc32(name.encode()), seed]).standard_normal(out[name].shape)
        drawn = base * np.exp(spread * noise) if base else spread * noise
        out[name] = jnp.asarray(drawn.astype(out[name].dtype))
    for name, factor in factors.items():
        out[name] = (out[name] * factor).astype(out[name].dtype)
    return out
```

```python
from contextlib import ExitStack

import concourse.bass as bass
from concourse import mybir

ALU = mybir.AluOpType
ACT = mybir.ActivationFunctionType
AX = mybir.AxisListType
F32 = mybir.dt.float32
F32R = mybir.dt.float32r
BF16 = mybir.dt.bfloat16
I32 = mybir.dt.int32
U32 = mybir.dt.uint32

P = 128
SUB = 2
AHEAD = 6

BLOCK = 32
E4M3_MAX = 448.0
E4M3_EMAX = 8
ROUND_GAIN = float(2 ** 20)
ROUND_FLOOR = 1.5 * 2.0 ** -6 * ROUND_GAIN
EXP_MASK = 0x7F800000
MANTISSA = 1 << 23
AMAX_FLOOR = 2.0 ** (E4M3_EMAX - 126)


def adaln_attn_ffn_kernel(
    nc: bass.Bass,
    x: bass.AP,
    condition: bass.AP,
    length: bass.AP,
    cond_w: bass.AP,
    wqkv: bass.AP,
    bqkv: bass.AP,
    wo: bass.AP,
    bo: bass.AP,
    conv_w: bass.AP,
    ffn_w: bass.AP,
    ffn_b: bass.AP,
    out: bass.AP,
):
    B, C, T = x.shape
    D = wo.shape[0]
    N = ffn_w.shape[0]
    TAPS = conv_w.shape[2]
    JB = P // C
    TILES = B * C // P
    UNITS = TILES // SUB
    TC = T // P
    NB = T // BLOCK
    TOK = SUB * P
    WBLOCKS = N // TOK
    STEPS = UNITS + WBLOCKS
    QSCALE = float(D) ** -0.5
    assert C == 32 and T == 512 and N == 512 and D == P and WBLOCKS == 2

    x_v = x.rearrange("(i j) c t -> i (j c) t", j=JB)
    out_v = out.rearrange("(i j) c t -> i (j c) t", j=JB)
    cond_w_v = cond_w.rearrange("k c d -> k c d")

    with ExitStack() as ctx:
        def sb(name, shape, dt):
            return ctx.enter_context(nc.sbuf_tensor(name, shape, dt))

        def pb(name, shape, dt):
            return ctx.enter_context(nc.psum_tensor(name, shape, dt))

        def sem(name):
            return ctx.enter_context(nc.semaphore(name))

        wqkv_f = sb("wqkv_f", [P, TC, 3 * D], F32)
        wqkv_hi = sb("wqkv_hi", [P, TC, 3 * D], F32R)
        wqkv_lo = sb("wqkv_lo", [P, TC, 3 * D], F32R)
        wo_f = sb("wo_f", [P, T], F32)
        wo_hi = sb("wo_hi", [P, T], F32R)
        wo_lo = sb("wo_lo", [P, T], F32R)
        ffn_w_f = sb("ffn_w_f", [P, N // P, T], F32)
        wq_t = sb("wq_t", [P, TC, N], BF16)
        bqkv_sb = sb("bqkv_sb", [P, 3], F32)
        bq_scaled = sb("bq_scaled", [P, 1], F32)
        bo_row = sb("bo_row", [P, 1, T], F32)
        bias_row = sb("bias_row", [P, N], F32)
        bias_part = sb("bias_part", [P, 3, N], BF16)
        bias_rest = sb("bias_rest", [P, 2, N], F32)
        bias_rows = sb("bias_rows", [P, N], BF16)
        ones = sb("ones", [P, P], BF16)
        ident = sb("ident", [P, P], BF16)
        part_f = sb("part_f", [P, 1], F32)
        part_i = sb("part_i", [P, 1], I32)
        pos_i = sb("pos_i", [P, T], I32)
        pos_f = sb("pos_f", [P, T], F32)
        diag_i = sb("diag_i", [P, P], I32)
        diag_f = sb("diag_f", [P, P], F32)
        same = sb("same", [P, P], F32)
        taps = sb("taps", [P, TAPS], F32)
        band_k = sb("band_k", [P, TAPS, P], F32)
        band = sb("band", [P, P], F32)
        cond_row = sb("cond_row", [1, B], I32)
        len_i = sb("len_i", [P, B], I32)
        len_f = sb("len_f", [P, TILES], F32)
        len_inv = sb("len_inv", [P, TILES], F32)
        neg_len_inv = sb("neg_len_inv", [P, TILES], F32)

        x_sb = sb("x_sb", [P, UNITS, SUB, T], F32)
        mix_w = sb("mix_w", [P, UNITS, SUB, P], F32)

        mix_f = sb("mix_f", [P, 2, TC, TOK], F32)
        xc_hi = sb("xc_hi", [P, 2, TC, TOK], F32R)
        xc_lo = sb("xc_lo", [P, 2, TC, TOK], F32R)
        q_t = sb("q_t", [P, 2, TOK], F32)
        k_t = sb("k_t", [P, 2, TOK], F32)
        v_t = sb("v_t", [P, TOK], F32)
        v_sb = sb("v_sb", [P, 2, SUB, D], F32)
        ident_f = sb("ident_f", [P, P], F32)
        xb = sb("xb", [P, 2, SUB, T], F32)
        x2 = sb("x2", [P, 3, SUB, T], F32)
        eg = sb("eg", [P, 2, SUB], F32)
        negmax = sb("negmax", [P, SUB], F32)
        prob = sb("prob", [P, SUB, C], F32)
        psum_row = sb("psum_row", [P, SUB], F32)
        prob_inv = sb("prob_inv", [P, SUB], F32)
        prob_n = sb("prob_n", [P, SUB, C], F32)
        prob_t = sb("prob_t", [P, SUB, P], F32)
        o_hi = sb("o_hi", [P, TOK], F32R)
        o_lo = sb("o_lo", [P, TOK], F32R)
        masked = sb("masked", [P, SUB, T], F32)
        ysum = sb("ysum", [P, SUB], F32)
        gate_den = sb("gate_den", [P, SUB], F32)
        gate = sb("gate", [P, SUB], F32)
        amax = sb("amax", [P, 2, SUB, NB], F32)
        amax_g = sb("amax_g", [P, SUB, NB], F32)
        amax_e = sb("amax_e", [P, SUB, NB], F32)
        scale = sb("scale", [P, 2, SUB, NB], F32)
        inv = sb("inv", [P, SUB, NB], F32)
        inv_g = sb("inv_g", [P, SUB, NB], F32)
        h = sb("h", [P, 2, SUB, T], F32)
        h_mag = sb("h_mag", [P, 2, SUB, T], BF16)
        h_sum = sb("h_sum", [P, SUB, T], F32)
        h_round = sb("h_round", [P, SUB, T], BF16)
        h_clip = sb("h_clip", [P, 2, SUB, T], BF16)
        xq = sb("xq", [P, 2, SUB, T], BF16)
        xq_t = sb("xq_t", [P, 2, TC, TOK], BF16)
        ffn_out = sb("ffn_out", [P, SUB, N], BF16)
        result = sb("result", [P, SUB, T], F32)

        ps_mix = [pb(f"ps_mix{t}", [P, TC, P], F32) for t in range(SUB)]
        ps_qk = pb("ps_qk", [P, 2, TOK], F32)
        ps_v = pb("ps_v", [P, TOK], F32)
        ps_att = pb("ps_att", [P, 512], F32)
        ps_s = ps_att[:, 0:SUB * C].rearrange("p (t k) -> p t k", t=SUB)
        ps_o = ps_att[:, 0:TOK]
        ps_wo = pb("ps_wo", [P, T], F32)
        ps_conv = ps_wo[:, 0:SUB]
        ps_tr = pb("ps_tr", [P, TC, TOK], BF16)
        ps_ffn = pb("ps_ffn", [P, N], F32)

        x_loaded = [sem(f"x_loaded{u}") for u in range(UNITS)]
        cond_loaded = sem("cond_loaded")
        mix_w_loaded = [sem(f"mix_w_loaded{i}") for i in range(TILES)]
        wqkv_loaded = sem("wqkv_loaded")
        bqkv_loaded = sem("bqkv_loaded")
        wo_loaded = sem("wo_loaded")
        bo_loaded = sem("bo_loaded")
        ffn_w_loaded = [sem(f"ffn_w_loaded{v}") for v in range(WBLOCKS)]
        bias_loaded = sem("bias_loaded")
        taps_loaded = sem("taps_loaded")
        len_loaded = sem("len_loaded")
        stored = [sem(f"stored{t}") for t in range(SUB)]
        mix_w_zeroed = sem("mix_w_zeroed")
        iota_done = sem("iota_done")
        iota_f_done = sem("iota_f_done")
        same_zeroed = sem("same_zeroed")
        same_done = sem("same_done")
        prob_t_zeroed = sem("prob_t_zeroed")
        ident_done = sem("ident_done")
        ones_done = sem("ones_done")
        band_parts = sem("band_parts")
        band_sums = sem("band_sums")
        band_done = sem("band_done")
        len_f_done = sem("len_f_done")
        len_inv_done = sem("len_inv_done")
        neg_len_done = sem("neg_len_done")
        wqkv_hi_done = sem("wqkv_hi_done")
        wqkv_lo_done = sem("wqkv_lo_done")
        wo_hi_done = sem("wo_hi_done")
        wo_lo_done = sem("wo_lo_done")
        bq_done = sem("bq_done")
        bias_chain = sem("bias_chain")
        bias_done = sem("bias_done")
        mix_done = sem("mix_done")
        xc_hi_done = sem("xc_hi_done")
        mix_f_done = sem("mix_f_done")
        xc_lo_done = sem("xc_lo_done")
        exp_done = sem("exp_done")
        wo_done = sem("wo_done")
        x2_done = sem("x2_done")
        ysum_done = sem("ysum_done")
        gate_exp_done = sem("gate_exp_done")
        ffn_done = sem("ffn_done")
        ffn_out_done = sem("ffn_out_done")
        result_done = sem("result_done")
        qk_done = sem("qk_done")
        v_done = sem("v_done")
        q_copied = sem("q_copied")
        k_copied = sem("k_copied")
        v_t_copied = sem("v_t_copied")
        v_turned = sem("v_turned")
        v_copied = sem("v_copied")
        scores_done = sem("scores_done")
        negmax_done = sem("negmax_done")
        prob_inv_done = sem("prob_inv_done")
        prob_n_done = sem("prob_n_done")
        prob_t_done = sem("prob_t_done")
        pv_done = sem("pv_done")
        o_hi_done = sem("o_hi_done")
        o_lo_done = sem("o_lo_done")
        xb_done = sem("xb_done")
        conv_done = sem("conv_done")
        gate_den_done = sem("gate_den_done")
        gate_done = sem("gate_done")
        amax_g_done = sem("amax_g_done")
        inv_g_done = sem("inv_g_done")
        amax_done = sem("amax_done")
        amax_e_done = sem("amax_e_done")
        scale_done = sem("scale_done")
        inv_done = sem("inv_done")
        h_done = sem("h_done")
        h_mag_done = sem("h_mag_done")
        h_sum_done = sem("h_sum_done")
        h_round_done = sem("h_round_done")
        h_clip_done = sem("h_clip_done")
        xq_done = sem("xq_done")
        tr_done = sem("tr_done")
        xq_t_done = sem("xq_t_done")

        block = ctx.enter_context(nc.Block())

        def is_unit(u):
            return 0 <= u < UNITS

        def gather_mix_w(queue, u, t):
            i = SUB * u + t
            for j in range(JB):
                b = i * JB + j
                k = queue.value_load(cond_row[0:1, b:b + 1], min_val=0,
                                     max_val=cond_w.shape[0] - 1)
                queue.dma_start(mix_w[C * j:C * (j + 1), u, t, C * j:C * (j + 1)],
                                cond_w[bass.ds(k, 1)].rearrange("k c d -> (k c) d")) \
                    .then_inc(mix_w_loaded[i], 16)

        @block.sync
        def _(sp):
            def load_x(u, t):
                nc.sync.dma_start(x_sb[:, u, t, :], x_v[SUB * u + t]).then_inc(x_loaded[u], 16)

            def store(u):
                for t in range(SUB):
                    sp.wait_ge(result_done, SUB * u + t + 1)
                    nc.sync.dma_start(out_v[SUB * u + t], result[:, t, :]) \
                        .then_inc(stored[t], 16)

            nc.sync.dma_start(cond_row[:], condition.rearrange("(a b) -> a b", a=1)) \
                .then_inc(cond_loaded, 16)
            load_x(0, 0)
            load_x(0, 1)
            sp.wait_ge(cond_loaded, 16)
            sp.wait_ge(mix_w_zeroed, 1)
            gather_mix_w(nc.sync, 0, 0)
            for u in range(1, UNITS):
                nc.sync.dma_start(x_sb[:, u], x_v[SUB * u:SUB * (u + 1)].rearrange("i p t -> p i t")) \
                    .then_inc(x_loaded[u], 32)
                for t in range(SUB):
                    gather_mix_w(nc.sync, u, t)
                if u >= AHEAD:
                    store(u - AHEAD)
            for u in range(UNITS - AHEAD, UNITS):
                store(u)
            for t in range(SUB):
                sp.wait_ge(stored[t], 16 * UNITS)

        @block.gpsimd
        def _(pool):
            nc.gpsimd.dma_start(len_i[:], length.partition_broadcast(P)).then_inc(len_loaded, 16)
            nc.gpsimd.dma_start(taps[:], conv_w.rearrange("a b k -> (a b k)").partition_broadcast(P)) \
                .then_inc(taps_loaded, 16)
            nc.gpsimd.iota(diag_i[:], [[-1, P]], base=TAPS // 2, channel_multiplier=1) \
                .then_inc(iota_done, 1)
            nc.gpsimd.iota(part_i[:], [[1, 1]], channel_multiplier=1).then_inc(iota_done, 1)
            nc.gpsimd.iota(pos_i[:], [[1, T]], channel_multiplier=0).then_inc(iota_done, 1)
            pool.wait_ge(cond_loaded, 16)
            pool.wait_ge(mix_w_zeroed, 1)
            gather_mix_w(nc.gpsimd, 0, 1)
            nc.gpsimd.dma_start(bias_row[:], ffn_b.partition_broadcast(P)).then_inc(bias_loaded, 16)
            nc.gpsimd.dma_start(bo_row[:, 0, :], bo.partition_broadcast(P)).then_inc(bo_loaded, 16)
            nc.gpsimd.memset(prob_t[:], 0.0).then_inc(prob_t_zeroed, 1)
            nc.gpsimd.memset(ones[:], 1.0).then_inc(ones_done, 1)

            def residual(u):
                pool.wait_ge(x_loaded[u], 32)
                if u == 0:
                    pool.wait_ge(bo_loaded, 16)
                if u >= 2:
                    pool.wait_ge(x2_done, SUB * (u - 1))
                nc.gpsimd.tensor_tensor(xb[:, u % 2], x_sb[:, u],
                                        bo_row[:].to_broadcast([P, SUB, T]), ALU.add) \
                    .then_inc(xb_done, 1)

            def split_mix_lo(u, t):
                if u >= 2 and t == 0:
                    pool.wait_ge(v_done, u - 1)
                pool.wait_ge(mix_f_done, SUB * u + t + 1)
                tok = slice(t * P, (t + 1) * P)
                nc.gpsimd.tensor_tensor(xc_lo[:, u % 2, :, tok], mix_f[:, u % 2, :, tok],
                                        xc_hi[:, u % 2, :, tok].bitcast(F32), ALU.subtract) \
                    .then_inc(xc_lo_done, 1)

            def dequantise(v):
                pool.wait_ge(h_clip_done, v + 1)
                pool.wait_ge(scale_done, v + 1)
                if v >= 2:
                    pool.wait_ge(tr_done, v - 1)
                nc.gpsimd.tensor_tensor(
                    xq[:, v % 2].rearrange("p t (n k) -> p (t n) k", k=BLOCK),
                    h_clip[:, v % 2].rearrange("p t (n k) -> p (t n) k", k=BLOCK),
                    scale[:, v % 2].rearrange("p t n -> p (t n)").unsqueeze(2)
                    .to_broadcast([P, SUB * NB, BLOCK]), ALU.mult).then_inc(xq_done, 1)

            def final_sum(u, t):
                pool.wait_ge(ffn_out_done, SUB * u + t + 1)
                pool.wait_ge(x2_done, SUB * u + t + 1)
                if u >= 1:
                    pool.wait_ge(stored[t], 16 * u)
                nc.gpsimd.tensor_tensor(result[:, t, :], ffn_out[:, t, :], x2[:, u % 3, t, :],
                                        ALU.add).then_inc(result_done, 1)

            for u in range(2):
                for t in range(SUB):
                    split_mix_lo(u, t)
            dequantise(0)
            for s in range(STEPS):
                if is_unit(s):
                    residual(s)
                if is_unit(s - 2):
                    final_sum(s - 2, 0)
                if is_unit(s + 2):
                    split_mix_lo(s + 2, 0)
                if s + 1 < STEPS:
                    dequantise(s + 1)
                if is_unit(s + 2):
                    split_mix_lo(s + 2, 1)
                if is_unit(s - 2):
                    final_sum(s - 2, 1)

        @block.tensor
        def _(pe):
            def mix(u):
                for t in range(SUB):
                    pe.wait_ge(x_loaded[u], 32)
                    pe.wait_ge(mix_w_loaded[SUB * u + t], 16 * JB)
                    if u >= 1:
                        pe.wait_ge(mix_f_done, SUB * (u - 1) + t + 1)
                    for c in range(TC):
                        mm = nc.tensor.matmul(ps_mix[t][:, c, :], x_sb[:, u, t, c * P:(c + 1) * P],
                                              mix_w[:, u, t, :], start=True, stop=True)
                    mm.then_inc(mix_done, 1)

            def passes(u):
                hi, lo = xc_hi[:, u % 2], xc_lo[:, u % 2]
                return [(a, b, c) for a, b in ((wqkv_hi, hi), (wqkv_lo, hi), (wqkv_hi, lo))
                        for c in range(TC)]

            def project_qk(u, which):
                if which == 0:
                    if u == 0:
                        pe.wait_ge(wqkv_hi_done, 1)
                        pe.wait_ge(wqkv_lo_done, 1)
                    else:
                        pe.wait_ge(k_copied, u)
                    pe.wait_ge(xc_hi_done, SUB * (u + 1))
                steps = passes(u)
                for n, (w, xt, c) in enumerate(steps):
                    if n == 2 * TC and which == 0:
                        pe.wait_ge(xc_lo_done, SUB * (u + 1))
                    mm = nc.tensor.matmul(ps_qk[:, which, :], w[:, c, which * D:(which + 1) * D],
                                          xt[:, c, :], start=(n == 0), stop=(n == len(steps) - 1))
                if which == 1:
                    mm.then_inc(qk_done, 1)

            def project_v(u):
                if u >= 1:
                    pe.wait_ge(v_copied, u)
                steps = passes(u)
                for n, (w, xt, c) in enumerate(steps):
                    mm = nc.tensor.matmul(ps_v[:], w[:, c, 2 * D:3 * D], xt[:, c, :],
                                          start=(n == 0), stop=(n == len(steps) - 1))
                mm.then_inc(v_done, 1)

            def turn_v(u):
                if u == 0:
                    pe.wait_ge(ident_done, 2)
                pe.wait_ge(v_t_copied, u + 1)
                for t in range(SUB):
                    tok = slice(t * P, (t + 1) * P)
                    mm = nc.tensor.transpose(ps_v[:, tok], v_t[:, tok], ident_f[:])
                mm.then_inc(v_turned, 1)

            def scores(u):
                pe.wait_ge(q_copied, u + 1)
                pe.wait_ge(k_copied, u + 1)
                if u >= 1:
                    pe.wait_ge(o_hi_done, u)
                    pe.wait_ge(o_lo_done, u)
                for t in range(SUB):
                    for j in range(JB):
                        tok = slice(t * P + j * C, t * P + (j + 1) * C)
                        mm = nc.tensor.matmul(ps_s[j * C:(j + 1) * C, t, :], q_t[:, u % 2, tok],
                                              k_t[:, u % 2, tok], start=True, stop=True)
                mm.then_inc(scores_done, 1)

            def attend(u):
                pe.wait_ge(v_copied, u + 1)
                pe.wait_ge(prob_t_done, JB * (u + 1))
                pe.wait_ge(exp_done, SUB * (u + 1))
                for t in range(SUB):
                    mm = nc.tensor.matmul(ps_o[:, t * P:(t + 1) * P], v_sb[:, u % 2, t, :],
                                          prob_t[:, t, :], start=True, stop=True)
                mm.then_inc(pv_done, 1)

            def project_out(u, t):
                if u == 0 and t == 0:
                    pe.wait_ge(wo_hi_done, 1)
                    pe.wait_ge(wo_lo_done, 1)
                if t == 0:
                    pe.wait_ge(o_hi_done, u + 1)
                    pe.wait_ge(o_lo_done, u + 1)
                if t == 0 and u > 0:
                    pe.wait_ge(gate_exp_done, SUB * u)
                if t > 0:
                    pe.wait_ge(x2_done, SUB * u + t)
                tok = slice(t * P, (t + 1) * P)
                for n, (o, w) in enumerate(((o_hi, wo_hi), (o_hi, wo_lo), (o_lo, wo_hi))):
                    mm = nc.tensor.matmul(ps_wo[:], o[:, tok], w[:], start=(n == 0), stop=(n == 2))
                mm.then_inc(wo_done, 1)

            def convolve(u):
                if u == 0:
                    pe.wait_ge(band_done, 1)
                pe.wait_ge(ysum_done, SUB * (u + 1))
                nc.tensor.matmul(ps_conv, band[:], ysum[:], start=True, stop=True) \
                    .then_inc(conv_done, 1)

            def transpose(v):
                if v == 0:
                    pe.wait_ge(ident_done, 1)
                pe.wait_ge(xq_done, v + 1)
                if v >= 1:
                    pe.wait_ge(xq_t_done, v)
                for c in range(TC):
                    for t in range(SUB):
                        mm = nc.tensor.transpose(ps_tr[:, c, t * P:(t + 1) * P],
                                                 xq[:, v % 2, t, c * P:(c + 1) * P], ident[:])
                mm.then_inc(tr_done, 1)

            def ffn(u, t):
                if u == 0 and t == 0:
                    pe.wait_ge(bias_done, 1)
                    pe.wait_ge(ones_done, 1)
                pe.wait_ge(xq_t_done, WBLOCKS + u + 1)
                if u > 0 or t > 0:
                    pe.wait_ge(ffn_out_done, SUB * u + t)
                nc.tensor.matmul(ps_ffn[:], ones[:], bias_rows[:], start=True, stop=False)
                for c in range(TC):
                    mm = nc.tensor.matmul(ps_ffn[:], xq_t[:, u % 2, c, t * P:(t + 1) * P],
                                          wq_t[:, c, :], start=False, stop=(c == TC - 1))
                mm.then_inc(ffn_done, 1)

            mix(0)
            project_qk(0, 0)
            project_qk(0, 1)
            project_v(0)
            mix(1)
            for s in range(STEPS):
                if is_unit(s):
                    scores(s)
                    turn_v(s)
                transpose(s)
                if is_unit(s + 1):
                    project_qk(s + 1, 0)
                if is_unit(s):
                    attend(s)
                if is_unit(s - 2):
                    ffn(s - 2, 0)
                if is_unit(s):
                    project_out(s, 0)
                if is_unit(s + 2):
                    mix(s + 2)
                if is_unit(s):
                    project_out(s, 1)
                if is_unit(s - 2):
                    ffn(s - 2, 1)
                if is_unit(s + 1):
                    project_qk(s + 1, 1)
                    project_v(s + 1)
                if is_unit(s):
                    convolve(s)

        @block.scalar
        def _(act):
            nc.scalar.dma_start(wqkv_f[:], wqkv.rearrange("(c p) f -> p c f", p=P)) \
                .then_inc(wqkv_loaded, 16)
            nc.scalar.dma_start(ffn_w_f[:, 0:SUB], ffn_w[0:TOK].rearrange("(n p) t -> p n t", p=P)) \
                .then_inc(ffn_w_loaded[0], 16)
            nc.scalar.dma_start(bqkv_sb[:], bqkv.rearrange("(k d) -> d k", d=D),
                                allow_slow_non_contiguous=True).then_inc(bqkv_loaded, 16)

            def late_loads():
                nc.scalar.dma_start(wo_f[:], wo).then_inc(wo_loaded, 16)
                nc.scalar.dma_start(ffn_w_f[:, SUB:2 * SUB],
                                    ffn_w[TOK:2 * TOK].rearrange("(n p) t -> p n t", p=P)) \
                    .then_inc(ffn_w_loaded[1], 16)

            def split_weights():
                act.wait_ge(wqkv_loaded, 16)
                nc.scalar.activation(wqkv_hi[:], wqkv_f[:], ACT.Copy).then_inc(wqkv_hi_done, 1)
                act.wait_ge(bqkv_loaded, 16)
                nc.scalar.mul(bq_scaled[:], bqkv_sb[:, 0:1], QSCALE).then_inc(bq_done, 1)

            def split_wo():
                act.wait_ge(wo_loaded, 16)
                nc.scalar.activation(wo_hi[:], wo_f[:], ACT.Copy).then_inc(wo_hi_done, 1)

            def exp_scores(u):
                act.wait_ge(negmax_done, u + 1)
                if u >= 1:
                    act.wait_ge(prob_n_done, u)
                for t in range(SUB):
                    nc.scalar.activation(prob[:, t, :], ps_s[:, t, :], ACT.Exp,
                                         bias=negmax[:, t:t + 1],
                                         accum_out=psum_row[:, t:t + 1]).then_inc(exp_done, 1)

            def copy_mix(u):
                if u >= 2:
                    act.wait_ge(v_done, u - 1)
                    act.wait_ge(xc_lo_done, SUB * (u - 1))
                for t in range(SUB):
                    act.wait_ge(mix_done, SUB * u + t + 1)
                    tok = slice(t * P, (t + 1) * P)
                    nc.scalar.activation(xc_hi[:, u % 2, :, tok], ps_mix[t][:], ACT.Copy) \
                        .then_inc(xc_hi_done, 1)
                    nc.scalar.activation(mix_f[:, u % 2, :, tok], ps_mix[t][:], ACT.Copy) \
                        .then_inc(mix_f_done, 1)

            def magnitude(v):
                if v >= 2:
                    act.wait_ge(h_round_done, v - 1)
                for t in range(SUB):
                    act.wait_ge(h_done, SUB * v + t + 1)
                    nc.scalar.activation(h_mag[:, v % 2, t, :], h[:, v % 2, t, :], ACT.Abs,
                                         scale=ROUND_GAIN).then_inc(h_mag_done, 1)

            def copy_o_hi(u):
                act.wait_ge(pv_done, u + 1)
                if u >= 1:
                    act.wait_ge(wo_done, SUB * u)
                nc.scalar.activation(o_hi[:], ps_o, ACT.Copy).then_inc(o_hi_done, 1)

            def copy_qkv(u):
                act.wait_ge(qk_done, u + 1)
                if u == 0:
                    act.wait_ge(bq_done, 1)
                if u >= 2:
                    act.wait_ge(scores_done, u - 1)
                nc.scalar.activation(q_t[:, u % 2], ps_qk[:, 0, :], ACT.Identity,
                                     bias=bq_scaled[:], scale=QSCALE).then_inc(q_copied, 1)
                nc.scalar.activation(k_t[:, u % 2], ps_qk[:, 1, :], ACT.Identity,
                                     bias=bqkv_sb[:, 1:2]).then_inc(k_copied, 1)
                act.wait_ge(v_done, u + 1)
                if u >= 1:
                    act.wait_ge(v_turned, u)
                nc.scalar.activation(v_t[:], ps_v[:], ACT.Identity, bias=bqkv_sb[:, 2:3]) \
                    .then_inc(v_t_copied, 1)

            def copy_v(u):
                act.wait_ge(v_turned, u + 1)
                if u >= 2:
                    act.wait_ge(pv_done, u - 1)
                nc.scalar.activation(v_sb[:, u % 2], ps_v[:].rearrange("p (t d) -> p t d", t=SUB),
                                     ACT.Copy).then_inc(v_copied, 1)

            def exp_gate(u):
                act.wait_ge(conv_done, u + 1)
                if u == 0:
                    act.wait_ge(neg_len_done, 1)
                if u >= 2:
                    act.wait_ge(gate_den_done, u - 1)
                for t in range(SUB):
                    i = SUB * u + t
                    nc.scalar.activation(eg[:, u % 2, t:t + 1], ps_conv[:, t:t + 1], ACT.Exp,
                                         scale=neg_len_inv[:, i:i + 1]).then_inc(gate_exp_done, 1)

            def copy_transposed(v):
                act.wait_ge(tr_done, v + 1)
                if v >= WBLOCKS + 2:
                    act.wait_ge(ffn_done, SUB * (v - WBLOCKS - 1))
                dst = wq_t[:, :, v * TOK:(v + 1) * TOK] if v < WBLOCKS else xq_t[:, v % 2]
                nc.scalar.activation(dst, ps_tr[:], ACT.Copy).then_inc(xq_t_done, 1)

            def copy_ffn(u, t):
                act.wait_ge(ffn_done, SUB * u + t + 1)
                if u >= 1:
                    act.wait_ge(result_done, SUB * (u - 1) + t + 1)
                nc.scalar.activation(ffn_out[:, t, :], ps_ffn[:], ACT.Copy).then_inc(ffn_out_done, 1)

            split_weights()
            late_loads()
            copy_mix(0)
            magnitude(0)
            split_wo()
            copy_qkv(0)
            copy_mix(1)
            for s in range(STEPS):
                if is_unit(s):
                    exp_scores(s)
                    copy_v(s)
                copy_transposed(s)
                if is_unit(s):
                    copy_o_hi(s)
                if s + 1 < STEPS:
                    magnitude(s + 1)
                if is_unit(s - 2):
                    copy_ffn(s - 2, 0)
                if is_unit(s + 2):
                    copy_mix(s + 2)
                if is_unit(s - 2):
                    copy_ffn(s - 2, 1)
                if is_unit(s + 1):
                    copy_qkv(s + 1)
                if is_unit(s):
                    exp_gate(s)

        @block.vector
        def _(dve):
            def constants_a():
                dve.wait_ge(wqkv_loaded, 16)
                dve.wait_ge(wqkv_hi_done, 1)
                nc.vector.tensor_tensor(wqkv_lo[:], wqkv_f[:], wqkv_hi[:].bitcast(F32),
                                        ALU.subtract).then_inc(wqkv_lo_done, 1)

            def iotas():
                dve.wait_ge(iota_done, 3)
                nc.vector.tensor_copy(pos_f[:], pos_i[:]).then_inc(iota_f_done, 1)
                nc.vector.tensor_copy(part_f[:], part_i[:]).then_inc(iota_f_done, 1)
                nc.vector.tensor_copy(diag_f[:], diag_i[:]).then_inc(iota_f_done, 1)
                dve.wait_ge(iota_f_done, 3)
                nc.vector.tensor_scalar(ident[:], diag_f[:], float(TAPS // 2), None, ALU.is_equal) \
                    .then_inc(ident_done, 1)
                nc.vector.tensor_scalar(ident_f[:], diag_f[:], float(TAPS // 2), None,
                                        ALU.is_equal).then_inc(ident_done, 1)

            def lengths():
                dve.wait_ge(len_loaded, 16)
                for j in range(JB):
                    p = slice(j * C, (j + 1) * C)
                    nc.vector.tensor_copy(len_f[p, :],
                                          len_i[p, :].rearrange("p (i j) -> p i j", j=JB)[:, :, j]) \
                        .then_inc(len_f_done, 1)
                dve.wait_ge(len_f_done, JB)
                nc.vector.reciprocal(len_inv[:], len_f[:]).then_inc(len_inv_done, 1)
                dve.wait_ge(len_inv_done, 1)
                nc.vector.tensor_scalar(neg_len_inv[:], len_inv[:], -1.0, None, ALU.mult) \
                    .then_inc(neg_len_done, 1)

            def band_matrix():
                nc.vector.memset(same[:], 0.0).then_inc(same_zeroed, 1)
                dve.wait_ge(same_zeroed, 1)
                for j in range(JB):
                    p = slice(j * C, (j + 1) * C)
                    nc.vector.memset(same[p, p], 1.0).then_inc(same_done, 1)
                dve.wait_ge(taps_loaded, 16)
                for k in range(TAPS):
                    nc.vector.tensor_scalar(band_k[:, k, :], diag_f[:], float(k), taps[:, k:k + 1],
                                            ALU.is_equal, ALU.mult).then_inc(band_parts, 1)
                dve.wait_ge(band_parts, TAPS)
                dve.wait_ge(same_done, JB)
                for k in range(1, TAPS):
                    if k >= 2:
                        dve.wait_ge(band_sums, k - 1)
                    nc.vector.tensor_tensor(band_k[:, 0, :], band_k[:, 0, :], band_k[:, k, :],
                                            ALU.add).then_inc(band_sums, 1)
                dve.wait_ge(band_sums, TAPS - 1)
                nc.vector.tensor_tensor(band[:], band_k[:, 0, :], same[:], ALU.mult) \
                    .then_inc(band_done, 1)

            def split_wo():
                dve.wait_ge(wo_hi_done, 1)
                nc.vector.tensor_tensor(wo_lo[:], wo_f[:], wo_hi[:].bitcast(F32), ALU.subtract) \
                    .then_inc(wo_lo_done, 1)

            def split_bias():
                dve.wait_ge(bias_loaded, 16)
                rest = bias_row[:]
                n = 0
                for k in range(3):
                    nc.vector.tensor_copy(bias_part[:, k, :], rest).then_inc(bias_chain, 1)
                    n += 1
                    dve.wait_ge(bias_chain, n)
                    if k < 2:
                        nc.vector.tensor_tensor(bias_rest[:, k, :], rest, bias_part[:, k, :],
                                                ALU.subtract).then_inc(bias_chain, 1)
                        n += 1
                        dve.wait_ge(bias_chain, n)
                        rest = bias_rest[:, k, :]
                for k in range(3):
                    nc.vector.tensor_scalar(bias_part[:, k, :], bias_part[:, k, :],
                                            row_is[:, k:k + 1], None, ALU.mult) \
                        .then_inc(bias_chain, 1)
                n += 3
                dve.wait_ge(bias_chain, n)
                nc.vector.tensor_tensor(bias_part[:, 0, :], bias_part[:, 0, :], bias_part[:, 1, :],
                                        ALU.add).then_inc(bias_chain, 1)
                dve.wait_ge(bias_chain, n + 1)
                nc.vector.tensor_tensor(bias_rows[:], bias_part[:, 0, :], bias_part[:, 2, :],
                                        ALU.add).then_inc(bias_done, 1)

            def row_masks():
                for k in range(3):
                    nc.vector.tensor_scalar(row_is[:, k:k + 1], part_f[:], float(k), None,
                                            ALU.is_equal).then_inc(row_is_done, 1)
                dve.wait_ge(row_is_done, 3)

            def score_max(u):
                dve.wait_ge(scores_done, u + 1)
                if u >= 1:
                    dve.wait_ge(exp_done, SUB * u)
                nc.vector.tensor_reduce(negmax[:], ps_s, AX.X, ALU.max, negate=True) \
                    .then_inc(negmax_done, 1)

            def softmax_steps(u):
                dve.wait_ge(exp_done, SUB * (u + 1))
                nc.vector.reciprocal(prob_inv[:], psum_row[:]).then_inc(prob_inv_done, 1)
                yield
                dve.wait_ge(prob_inv_done, u + 1)
                nc.vector.tensor_tensor(prob_n[:], prob[:],
                                        prob_inv[:].unsqueeze(2).to_broadcast([P, SUB, C]),
                                        ALU.mult).then_inc(prob_n_done, 1)
                yield
                dve.wait_ge(prob_n_done, u + 1)
                if u == 0:
                    dve.wait_ge(prob_t_zeroed, 1)
                else:
                    dve.wait_ge(pv_done, u)
                for j in range(JB):
                    p = slice(j * C, (j + 1) * C)
                    nc.vector.transpose(prob_t[p, :, p], prob_n[p]).then_inc(prob_t_done, 1)

            def copy_o_lo(u):
                dve.wait_ge(o_hi_done, u + 1)
                nc.vector.tensor_tensor(o_lo[:], ps_o, o_hi[:].bitcast(F32), ALU.subtract) \
                    .then_inc(o_lo_done, 1)

            def residual_sum(u, t):
                if t == 0:
                    dve.wait_ge(xb_done, u + 1)
                if u >= 3:
                    dve.wait_ge(result_done, SUB * (u - 3) + t + 1)
                dve.wait_ge(wo_done, SUB * u + t + 1)
                nc.vector.tensor_tensor(x2[:, u % 3, t, :], ps_wo[:], xb[:, u % 2, t, :],
                                        ALU.add).then_inc(x2_done, 1)

            def masked_sums(u):
                if u >= 1:
                    dve.wait_ge(conv_done, u)
                for t in range(SUB):
                    i = SUB * u + t
                    dve.wait_ge(x2_done, i + 1)
                    nc.vector.scalar_tensor_tensor(out=masked[:, t, :], in0=pos_f[:],
                                                   scalar=len_f[:, i:i + 1], in1=x2[:, u % 3, t, :],
                                                   op0=ALU.is_lt, op1=ALU.mult,
                                                   accum_out=ysum[:, t:t + 1]) \
                        .then_inc(ysum_done, 1)

            def block_max(v):
                if v < WBLOCKS:
                    dve.wait_ge(ffn_w_loaded[v], 16)
                    src = ffn_w_f[:, SUB * v:SUB * (v + 1)]
                else:
                    dve.wait_ge(x2_done, SUB * (v - WBLOCKS + 1))
                    src = x2[:, (v - WBLOCKS) % 3]
                nc.vector.tensor_reduce(amax[:, v % 2].rearrange("p t n -> p (t n)"),
                                        src.rearrange("p t (n k) -> p (t n) k", k=BLOCK),
                                        AX.X, ALU.max, apply_absolute_value=True) \
                    .then_inc(amax_done, 1)

            def gate_steps(v):
                u = v - WBLOCKS
                top = amax[:, v % 2]
                if v >= WBLOCKS:
                    g = gate[:].unsqueeze(2).to_broadcast([P, SUB, NB])
                    dve.wait_ge(gate_exp_done, SUB * (u + 1))
                    nc.vector.tensor_scalar(gate_den[:], eg[:, u % 2], 1.0, None, ALU.add) \
                        .then_inc(gate_den_done, 1)
                    yield
                    dve.wait_ge(gate_den_done, u + 1)
                    nc.vector.reciprocal(gate[:], gate_den[:]).then_inc(gate_done, 1)
                    yield
                    dve.wait_ge(gate_done, u + 1)
                    dve.wait_ge(amax_done, v + 1)
                    nc.vector.tensor_tensor(amax_g[:], top, g, ALU.mult).then_inc(amax_g_done, 1)
                    yield
                    dve.wait_ge(amax_g_done, u + 1)
                    top = amax_g[:]
                dve.wait_ge(amax_done, v + 1)
                nc.vector.tensor_scalar(amax_e[:].bitcast(U32), top.bitcast(U32), EXP_MASK, None,
                                        ALU.bitwise_and).then_inc(amax_e_done, 1)
                yield
                dve.wait_ge(amax_e_done, v + 1)
                if v >= 2:
                    dve.wait_ge(xq_done, v - 1)
                nc.vector.tensor_scalar(scale[:, v % 2], amax_e[:], AMAX_FLOOR,
                                        2.0 ** -E4M3_EMAX, ALU.max, ALU.mult) \
                    .then_inc(scale_done, 1)
                yield
                dve.wait_ge(scale_done, v + 1)
                nc.vector.tensor_scalar(inv[:].bitcast(I32), scale[:, v % 2].bitcast(I32), -1.0,
                                        float(254 * MANTISSA), ALU.mult, ALU.add) \
                    .then_inc(inv_done, 1)
                yield
                dve.wait_ge(inv_done, v + 1)
                if v >= WBLOCKS:
                    nc.vector.tensor_tensor(inv_g[:], inv[:], g, ALU.mult).then_inc(inv_g_done, 1)
                    yield
                    dve.wait_ge(inv_g_done, u + 1)

            def scaled(v):
                src = ffn_w_f[:, SUB * v:SUB * (v + 1)] if v < WBLOCKS else x2[:, (v - WBLOCKS) % 3]
                by = inv if v < WBLOCKS else inv_g
                for t in range(SUB):
                    nc.vector.tensor_tensor(
                        h[:, v % 2, t, :].rearrange("p (n k) -> p n k", k=BLOCK),
                        src[:, t, :].rearrange("p (n k) -> p n k", k=BLOCK),
                        by[:, t, :].unsqueeze(2).to_broadcast([P, NB, BLOCK]), ALU.mult) \
                        .then_inc(h_done, 1)

            def round_sum(v):
                for t in range(SUB):
                    dve.wait_ge(h_mag_done, SUB * v + t + 1)
                    nc.vector.scalar_tensor_tensor(out=h_sum[:, t, :], in0=h_mag[:, v % 2, t, :],
                                                   scalar=ROUND_FLOOR, in1=h[:, v % 2, t, :],
                                                   op0=ALU.max, op1=ALU.add) \
                        .then_inc(h_sum_done, 1)

            def round_back(v):
                dve.wait_ge(h_sum_done, SUB * (v + 1))
                nc.vector.scalar_tensor_tensor(out=h_round[:], in0=h_mag[:, v % 2],
                                               scalar=ROUND_FLOOR, in1=h_sum[:],
                                               op0=ALU.max, op1=ALU.subtract) \
                    .then_inc(h_round_done, 1)
                dve.wait_ge(h_round_done, v + 1)
                if v >= 2:
                    dve.wait_ge(xq_done, v - 1)
                nc.vector.tensor_scalar(h_clip[:, v % 2], h_round[:], E4M3_MAX, -E4M3_MAX,
                                        ALU.min, ALU.max).then_inc(h_clip_done, 1)

            row_is = sb("row_is", [P, 3], F32)
            row_is_done = sem("row_is_done")

            nc.vector.memset(mix_w[:], 0.0).then_inc(mix_w_zeroed, 1)
            iotas()
            row_masks()
            lengths()
            constants_a()

            def drained(steps):
                for _ in steps:
                    pass

            block_max(0)
            drained(gate_steps(0))
            scaled(0)
            round_sum(0)
            round_back(0)
            block_max(1)
            band_matrix()
            split_bias()
            for s in range(STEPS):
                small = [gate_steps(s + 1)] if s + 1 < STEPS else []
                if is_unit(s):
                    score_max(s)
                    if small:
                        next(small[0], None)
                        next(small[0], None)
                    small.append(softmax_steps(s))
                while small:
                    small = [c for c in small if next(c, 0) is None]
                if s == 0:
                    split_wo()
                if s + 1 < STEPS:
                    scaled(s + 1)
                if is_unit(s):
                    copy_o_lo(s)
                if s + 1 < STEPS:
                    round_sum(s + 1)
                if is_unit(s):
                    residual_sum(s, 0)
                if s + 1 < STEPS:
                    round_back(s + 1)
                if is_unit(s):
                    residual_sum(s, 1)
                    masked_sums(s)
                    block_max(s + WBLOCKS)


_INS = ['x', 'itok_B_0_15', 'itok_B_9_3973', 'L0_cond_weights', 'L0_attn_Wqkv', 'L0_attn_bqkv', 'L0_attn_Wo',
        'L0_attn_bo', 'L0_cond2_conv_w', 'L0_ffn_weight', 'L0_ffn_bias']
_OUTS = [((64, 32, 512), 'float32')]


def kernel(**inputs):
    import numpy as _np
    import concourse.bacc as _bacc
    from concourse import mybir as _mybir
    from concourse.bass_utils import run_bass_kernel_spmd as _run

    nc = _bacc.Bacc("TRN2", target_bir_lowering=False, num_devices=1)
    arrays, args = {}, []
    for name in _INS:
        a = _np.ascontiguousarray(inputs[name])
        arrays[f"in_{name}_dram"] = a
        args.append(nc.dram_tensor(f"in_{name}_dram", a.shape, _mybir.dt.from_np(a.dtype), kind="ExternalInput").ap())
    for i, (shape, dtype) in enumerate(_OUTS):
        dt = _mybir.dt.from_np(_np.dtype(dtype))
        args.append(nc.dram_tensor(f"out_{i}_dram", shape, dt, kind="ExternalOutput").ap())
    adaln_attn_ffn_kernel(nc, *args)
    r = _run(nc, [arrays], core_ids=[0])
    got = tuple(r.results[0][f"out_{i}_dram"] for i in range(len(_OUTS)))
    return got[0]
```

```python
from contextlib import ExitStack

import concourse.bass as bass
from concourse import mybir

ALU = mybir.AluOpType
ACT = mybir.ActivationFunctionType
AX = mybir.AxisListType
F32 = mybir.dt.float32
F32R = mybir.dt.float32r
BF16 = mybir.dt.bfloat16
I32 = mybir.dt.int32
U32 = mybir.dt.uint32

P = 128
SUB = 2
PART_ROWS = (0, 32, 64)
AHEAD = 5

BLOCK = 32
E4M3_MAX = 448.0
E4M3_EMAX = 8
ROUND_GAIN = float(2 ** 20)
ROUND_FLOOR = 1.5 * 2.0 ** -6 * ROUND_GAIN
EXP_MASK = 0x7F800000
MANTISSA = 1 << 23
AMAX_FLOOR = 2.0 ** (E4M3_EMAX - 126)


def adaln_attn_ffn_kernel(
    nc: bass.Bass,
    x: bass.AP,
    condition: bass.AP,
    length: bass.AP,
    cond_w: bass.AP,
    wqkv: bass.AP,
    bqkv: bass.AP,
    wo: bass.AP,
    bo: bass.AP,
    conv_w: bass.AP,
    ffn_w: bass.AP,
    ffn_b: bass.AP,
    out: bass.AP,
):
    B, C, T = x.shape
    D = wo.shape[0]
    N = ffn_w.shape[0]
    TAPS = conv_w.shape[2]
    JB = P // C
    TILES = B * C // P
    UNITS = TILES // SUB
    TC = T // P
    NB = T // BLOCK
    TOK = SUB * P
    WBLOCKS = N // TOK
    STEPS = UNITS + WBLOCKS
    QSCALE = float(D) ** -0.5
    assert C == 32 and T == 512 and N == 512 and D == P and WBLOCKS == 2

    x_v = x.rearrange("(i j) c t -> i (j c) t", j=JB)
    out_v = out.rearrange("(i j) c t -> i (j c) t", j=JB)
    cond_w_v = cond_w.rearrange("k c d -> k c d")

    with ExitStack() as ctx:
        def sb(name, shape, dt):
            return ctx.enter_context(nc.sbuf_tensor(name, shape, dt))

        def pb(name, shape, dt):
            return ctx.enter_context(nc.psum_tensor(name, shape, dt))

        def sem(name):
            return ctx.enter_context(nc.semaphore(name))

        wqkv_f = sb("wqkv_f", [P, TC, 3 * D], F32)
        wqkv_hi = sb("wqkv_hi", [P, TC, 3 * D], F32R)
        wqkv_lo = sb("wqkv_lo", [P, TC, 3 * D], F32R)
        wo_f = sb("wo_f", [P, T], F32)
        wo_hi = sb("wo_hi", [P, T], F32R)
        wo_lo = sb("wo_lo", [P, T], F32R)
        ffn_w_f = sb("ffn_w_f", [P, N // P, T], F32)
        wq_t = sb("wq_t", [P, TC, N], BF16)
        bqkv_sb = sb("bqkv_sb", [P, 3], F32)
        bq_scaled = sb("bq_scaled", [P, 1], F32)
        bo_row = sb("bo_row", [P, 1, T], F32)
        bias_row = sb("bias_row", [P, N], F32)
        bias_part = sb("bias_part", [P, 2, N], BF16)
        bias_rest = sb("bias_rest", [P, 2, N], F32)
        bias_rows = sb("bias_rows", [P, N], BF16)
        ones = sb("ones", [P, P], BF16)
        ident = sb("ident", [P, P], BF16)
        pos_i = sb("pos_i", [P, T], I32)
        pos_f = sb("pos_f", [P, T], F32)
        diag_i = sb("diag_i", [P, P], I32)
        diag_f = sb("diag_f", [P, P], F32)
        same = sb("same", [P, P], F32)
        taps = sb("taps", [P, TAPS], F32)
        band_k = sb("band_k", [P, TAPS, P], F32)
        band = sb("band", [P, P], F32)
        cond_row = sb("cond_row", [1, B], I32)
        len_i = sb("len_i", [P, B], I32)
        len_f = sb("len_f", [P, TILES], F32)
        len_inv = sb("len_inv", [P, TILES], F32)
        neg_len_inv = sb("neg_len_inv", [P, TILES], F32)

        x_sb = sb("x_sb", [P, UNITS, SUB, T], F32)
        mix_w = sb("mix_w", [P, UNITS, SUB, P], F32)

        mix_f = sb("mix_f", [P, 2, TC, TOK], F32)
        xc_hi = sb("xc_hi", [P, 2, TC, TOK], F32R)
        xc_lo = sb("xc_lo", [P, 2, TC, TOK], F32R)
        q_t = sb("q_t", [P, 2, TOK], F32)
        k_t = sb("k_t", [P, 2, TOK], F32)
        v_t = sb("v_t", [P, TOK], F32)
        v_sb = sb("v_sb", [P, 2, SUB, D], F32)
        ident_f = sb("ident_f", [P, P], F32)
        xb = sb("xb", [P, 2, SUB, T], F32)
        x2 = sb("x2", [P, 3, SUB, T], F32)
        eg = sb("eg", [P, 2, SUB], F32)
        negmax = sb("negmax", [P, SUB], F32)
        prob = sb("prob", [P, SUB, C], F32)
        psum_row = sb("psum_row", [P, SUB], F32)
        prob_inv = sb("prob_inv", [P, SUB], F32)
        prob_n = sb("prob_n", [P, SUB, C], F32)
        prob_t = sb("prob_t", [P, SUB, P], F32)
        o_hi = sb("o_hi", [P, TOK], F32R)
        o_lo = sb("o_lo", [P, TOK], F32R)
        masked = sb("masked", [P, SUB, T], F32)
        ysum = sb("ysum", [P, SUB], F32)
        gate_den = sb("gate_den", [P, SUB], F32)
        gate = sb("gate", [P, SUB], F32)
        amax = sb("amax", [P, 2, SUB, NB], F32)
        amax_g = sb("amax_g", [P, SUB, NB], F32)
        amax_e = sb("amax_e", [P, SUB, NB], F32)
        scale = sb("scale", [P, 2, SUB, NB], F32)
        inv = sb("inv", [P, SUB, NB], F32)
        inv_g = sb("inv_g", [P, SUB, NB], F32)
        h = sb("h", [P, 2, SUB, T], F32)
        h_mag = sb("h_mag", [P, 2, SUB, T], BF16)
        h_sum = sb("h_sum", [P, SUB, T], F32)
        h_round = sb("h_round", [P, SUB, T], BF16)
        h_clip = sb("h_clip", [P, 2, SUB, T], BF16)
        xq = sb("xq", [P, 2, SUB, T], BF16)
        xq_t = sb("xq_t", [P, 2, TC, TOK], BF16)
        ffn_out = sb("ffn_out", [P, SUB, N], BF16)
        result = sb("result", [P, SUB, T], F32)

        ps_mix = [pb(f"ps_mix{t}", [P, TC, P], F32) for t in range(SUB)]
        ps_qk = pb("ps_qk", [P, 2, TOK], F32)
        ps_v = pb("ps_v", [P, TOK], F32)
        ps_att = pb("ps_att", [P, 512], F32)
        ps_s = ps_att[:, 0:SUB * C].rearrange("p (t k) -> p t k", t=SUB)
        ps_o = ps_att[:, 0:TOK]
        ps_wo = pb("ps_wo", [P, T], F32)
        ps_conv = ps_wo[:, 0:SUB]
        ps_tr = pb("ps_tr", [P, TC, TOK], BF16)
        ps_ffn = pb("ps_ffn", [P, N], F32)

        x_loaded = [sem(f"x_loaded{u}") for u in range(UNITS)]
        cond_loaded = sem("cond_loaded")
        mix_w_loaded = [sem(f"mix_w_loaded{i}") for i in range(TILES)]
        wqkv_loaded = sem("wqkv_loaded")
        bqkv_loaded = sem("bqkv_loaded")
        wo_loaded = sem("wo_loaded")
        bo_loaded = sem("bo_loaded")
        ffn_w_loaded = [sem(f"ffn_w_loaded{v}") for v in range(WBLOCKS)]
        bias_loaded = sem("bias_loaded")
        taps_loaded = sem("taps_loaded")
        len_loaded = sem("len_loaded")
        stored = [sem(f"stored{t}") for t in range(SUB)]
        mix_w_zeroed = sem("mix_w_zeroed")
        iota_done = sem("iota_done")
        iota_f_done = sem("iota_f_done")
        same_zeroed = sem("same_zeroed")
        same_done = sem("same_done")
        prob_t_zeroed = sem("prob_t_zeroed")
        ident_done = sem("ident_done")
        ones_done = sem("ones_done")
        band_parts = sem("band_parts")
        band_sums = sem("band_sums")
        band_done = sem("band_done")
        len_f_done = sem("len_f_done")
        len_inv_done = sem("len_inv_done")
        neg_len_done = sem("neg_len_done")
        wqkv_hi_done = sem("wqkv_hi_done")
        wqkv_lo_done = sem("wqkv_lo_done")
        wo_hi_done = sem("wo_hi_done")
        wo_lo_done = sem("wo_lo_done")
        bq_done = sem("bq_done")
        bias_chain = sem("bias_chain")
        bias_done = sem("bias_done")
        bias_rows_zeroed = sem("bias_rows_zeroed")
        mix_done = sem("mix_done")
        xc_hi_done = sem("xc_hi_done")
        mix_f_done = sem("mix_f_done")
        xc_lo_done = sem("xc_lo_done")
        exp_done = sem("exp_done")
        wo_done = sem("wo_done")
        x2_done = sem("x2_done")
        ysum_done = sem("ysum_done")
        gate_exp_done = sem("gate_exp_done")
        ffn_done = sem("ffn_done")
        ffn_out_done = sem("ffn_out_done")
        result_done = sem("result_done")
        last_result_done = sem("last_result_done")
        qk_done = sem("qk_done")
        v_done = sem("v_done")
        q_copied = sem("q_copied")
        k_copied = sem("k_copied")
        v_t_copied = sem("v_t_copied")
        v_turned = sem("v_turned")
        v_copied = sem("v_copied")
        scores_done = sem("scores_done")
        negmax_done = sem("negmax_done")
        prob_inv_done = sem("prob_inv_done")
        prob_n_done = sem("prob_n_done")
        prob_t_done = sem("prob_t_done")
        pv_done = sem("pv_done")
        o_hi_done = sem("o_hi_done")
        o_lo_done = sem("o_lo_done")
        xb_done = sem("xb_done")
        conv_done = sem("conv_done")
        gate_den_done = sem("gate_den_done")
        gate_done = sem("gate_done")
        amax_g_done = sem("amax_g_done")
        inv_g_done = sem("inv_g_done")
        amax_done = sem("amax_done")
        amax_e_done = sem("amax_e_done")
        scale_done = sem("scale_done")
        inv_done = sem("inv_done")
        h_done = sem("h_done")
        h_mag_done = sem("h_mag_done")
        h_sum_done = sem("h_sum_done")
        h_round_done = sem("h_round_done")
        h_clip_done = sem("h_clip_done")
        xq_done = sem("xq_done")
        tr_done = sem("tr_done")
        xq_t_done = sem("xq_t_done")

        block = ctx.enter_context(nc.Block())

        def is_unit(u):
            return 0 <= u < UNITS

        def wo_bank(u, t):
            return ps_wo[:] if u < UNITS - 1 or t == 0 else ps_qk[:].rearrange("p k n -> p (k n)")

        def ffn_bank(u, t):
            return ps_ffn[:] if u < UNITS - 2 or t == 0 else \
                ps_mix[u - (UNITS - 2)][:].rearrange("p c k -> p (c k)")

        def turned(v, t0, t1):
            if v == STEPS - 1 and t0 == 1:
                return ps_v[:].bitcast(BF16).rearrange("p (c k) -> p c k", c=TC)
            return ps_tr[:, :, t0 * P:t1 * P]

        def wait_result(engine, u, t):
            if u < UNITS - 2:
                engine.wait_ge(result_done, SUB * u + t + 1)
            else:
                engine.wait_ge(last_result_done, SUB * (u - (UNITS - 2)) + t + 1)

        def final_sum(engine, u, t):
            engine.wait_ge(ffn_out_done, SUB * u + t + 1)
            engine.wait_ge(x2_done, SUB * u + t + 1)
            if u >= 1:
                engine.wait_ge(stored[t], 16 * u)
            engine.tensor_tensor(result[:, t, :], ffn_out[:, t, :], x2[:, u % 3, t, :],
                                 ALU.add) \
                .then_inc(result_done if u < UNITS - 2 else last_result_done, 1)

        def gather_mix_w(queue, u, t):
            i = SUB * u + t
            for j in range(JB):
                b = i * JB + j
                k = queue.value_load(cond_row[0:1, b:b + 1], min_val=0,
                                     max_val=cond_w.shape[0] - 1)
                queue.dma_start(mix_w[C * j:C * (j + 1), u, t, C * j:C * (j + 1)],
                                cond_w[bass.ds(k, 1)].rearrange("k c d -> (k c) d")) \
                    .then_inc(mix_w_loaded[i], 16)

        @block.sync
        def _(sp):
            def load_x(u, t):
                nc.sync.dma_start(x_sb[:, u, t, :], x_v[SUB * u + t]).then_inc(x_loaded[u], 16)

            def store(u):
                for t in range(SUB):
                    wait_result(sp, u, t)
                    nc.sync.dma_start(out_v[SUB * u + t], result[:, t, :]) \
                        .then_inc(stored[t], 16)

            nc.sync.dma_start(cond_row[:], condition.rearrange("(a b) -> a b", a=1)) \
                .then_inc(cond_loaded, 16)
            load_x(0, 0)
            load_x(0, 1)
            sp.wait_ge(cond_loaded, 16)
            sp.wait_ge(mix_w_zeroed, 1)
            gather_mix_w(nc.sync, 0, 0)
            for u in range(1, UNITS):
                nc.sync.dma_start(x_sb[:, u], x_v[SUB * u:SUB * (u + 1)].rearrange("i p t -> p i t")) \
                    .then_inc(x_loaded[u], 32)
                for t in range(SUB):
                    gather_mix_w(nc.sync, u, t)
                if u >= AHEAD:
                    store(u - AHEAD)
            for u in range(UNITS - AHEAD, UNITS):
                store(u)
            for t in range(SUB):
                sp.wait_ge(stored[t], 16 * UNITS)

        @block.gpsimd
        def _(pool):
            nc.gpsimd.dma_start(len_i[:], length.partition_broadcast(P)).then_inc(len_loaded, 16)
            nc.gpsimd.dma_start(taps[:], conv_w.rearrange("a b k -> (a b k)").partition_broadcast(P)) \
                .then_inc(taps_loaded, 16)
            nc.gpsimd.iota(diag_i[:], [[-1, P]], base=TAPS // 2, channel_multiplier=1) \
                .then_inc(iota_done, 1)
            nc.gpsimd.iota(pos_i[:], [[1, T]], channel_multiplier=0).then_inc(iota_done, 1)
            pool.wait_ge(cond_loaded, 16)
            pool.wait_ge(mix_w_zeroed, 1)
            gather_mix_w(nc.gpsimd, 0, 1)
            nc.gpsimd.memset(bias_rows[:], 0.0).then_inc(bias_rows_zeroed, 1)
            nc.gpsimd.memset(prob_t[:], 0.0).then_inc(prob_t_zeroed, 1)
            nc.gpsimd.memset(ones[:], 1.0).then_inc(ones_done, 1)

            def residual(u):
                pool.wait_ge(x_loaded[u], 32)
                if u == 0:
                    pool.wait_ge(bo_loaded, 16)
                if u >= 2:
                    pool.wait_ge(x2_done, SUB * (u - 1))
                nc.gpsimd.tensor_tensor(xb[:, u % 2], x_sb[:, u],
                                        bo_row[:].to_broadcast([P, SUB, T]), ALU.add) \
                    .then_inc(xb_done, 1)

            def split_mix_lo(u, t):
                if u >= 2 and t == 0:
                    pool.wait_ge(v_done, u - 1)
                pool.wait_ge(mix_f_done, SUB * u + t + 1)
                tok = slice(t * P, (t + 1) * P)
                nc.gpsimd.tensor_tensor(xc_lo[:, u % 2, :, tok], mix_f[:, u % 2, :, tok],
                                        xc_hi[:, u % 2, :, tok].bitcast(F32), ALU.subtract) \
                    .then_inc(xc_lo_done, 1)

            def dequantise(v, t0=0, t1=SUB):
                pool.wait_ge(h_clip_done, SUB * v + t1)
                pool.wait_ge(scale_done, v + 1)
                if v >= 2:
                    pool.wait_ge(tr_done, SUB * (v - 1))
                nc.gpsimd.tensor_tensor(
                    xq[:, v % 2, t0:t1].rearrange("p t (n k) -> p (t n) k", k=BLOCK),
                    h_clip[:, v % 2, t0:t1].rearrange("p t (n k) -> p (t n) k", k=BLOCK),
                    scale[:, v % 2, t0:t1].rearrange("p t n -> p (t n)").unsqueeze(2)
                    .to_broadcast([P, (t1 - t0) * NB, BLOCK]), ALU.mult) \
                    .then_inc(xq_done, t1 - t0)

            pool.wait_ge(wqkv_hi_done, 1)
            nc.gpsimd.tensor_tensor(wqkv_lo[:], wqkv_f[:], wqkv_hi[:].bitcast(F32),
                                    ALU.subtract).then_inc(wqkv_lo_done, 1)
            split_mix_lo(0, 0)
            split_mix_lo(0, 1)
            pool.wait_ge(wo_hi_done, 1)
            nc.gpsimd.tensor_tensor(wo_lo[:], wo_f[:], wo_hi[:].bitcast(F32), ALU.subtract) \
                .then_inc(wo_lo_done, 1)
            dequantise(0)
            split_mix_lo(1, 0)
            split_mix_lo(1, 1)
            for s in range(STEPS):
                if is_unit(s):
                    residual(s)
                if is_unit(s + 2):
                    split_mix_lo(s + 2, 0)
                if s + 1 < STEPS - 1:
                    dequantise(s + 1)
                elif s + 1 == STEPS - 1:
                    for t in range(SUB):
                        dequantise(s + 1, t, t + 1)
                if is_unit(s + 2):
                    split_mix_lo(s + 2, 1)
                if 0 <= s - 2 < UNITS - 2:
                    final_sum(nc.gpsimd, s - 2, 0)
                    final_sum(nc.gpsimd, s - 2, 1)

        @block.tensor
        def _(pe):
            def mix(u):
                for t in range(SUB):
                    pe.wait_ge(x_loaded[u], 32)
                    pe.wait_ge(mix_w_loaded[SUB * u + t], 16 * JB)
                    if u >= 1:
                        pe.wait_ge(mix_f_done, SUB * (u - 1) + t + 1)
                    for c in range(TC):
                        mm = nc.tensor.matmul(ps_mix[t][:, c, :], x_sb[:, u, t, c * P:(c + 1) * P],
                                              mix_w[:, u, t, :], start=True, stop=True)
                    mm.then_inc(mix_done, 1)

            def passes(u):
                hi, lo = xc_hi[:, u % 2], xc_lo[:, u % 2]
                return [(a, b, c) for a, b in ((wqkv_hi, hi), (wqkv_lo, hi), (wqkv_hi, lo))
                        for c in range(TC)]

            def project_qk(u, which, first=0, last=3):
                if which == 0 and first == 0:
                    if u == 0:
                        pe.wait_ge(wqkv_hi_done, 1)
                        pe.wait_ge(wqkv_lo_done, 1)
                    else:
                        pe.wait_ge(k_copied, u)
                    pe.wait_ge(xc_hi_done, SUB * (u + 1))
                steps = passes(u)
                for n in range(first * TC, last * TC):
                    w, xt, c = steps[n]
                    if n == 2 * TC and which == 0:
                        pe.wait_ge(xc_lo_done, SUB * (u + 1))
                    mm = nc.tensor.matmul(ps_qk[:, which, :], w[:, c, which * D:(which + 1) * D],
                                          xt[:, c, :], start=(n == 0), stop=(n == len(steps) - 1))
                if which == 1:
                    mm.then_inc(qk_done, 1)

            def project_v(u):
                if u >= 1:
                    pe.wait_ge(v_copied, u)
                steps = passes(u)
                for n, (w, xt, c) in enumerate(steps):
                    mm = nc.tensor.matmul(ps_v[:], w[:, c, 2 * D:3 * D], xt[:, c, :],
                                          start=(n == 0), stop=(n == len(steps) - 1))
                mm.then_inc(v_done, 1)

            def turn_v(u):
                if u == 0:
                    pe.wait_ge(ident_done, 2)
                pe.wait_ge(v_t_copied, u + 1)
                for t in range(SUB):
                    tok = slice(t * P, (t + 1) * P)
                    mm = nc.tensor.transpose(ps_v[:, tok], v_t[:, tok], ident_f[:])
                mm.then_inc(v_turned, 1)

            def scores(u):
                pe.wait_ge(q_copied, u + 1)
                pe.wait_ge(k_copied, u + 1)
                if u >= 1:
                    pe.wait_ge(o_hi_done, u)
                    pe.wait_ge(o_lo_done, u)
                for t in range(SUB):
                    for j in range(JB):
                        tok = slice(t * P + j * C, t * P + (j + 1) * C)
                        mm = nc.tensor.matmul(ps_s[j * C:(j + 1) * C, t, :], q_t[:, u % 2, tok],
                                              k_t[:, u % 2, tok], start=True, stop=True)
                mm.then_inc(scores_done, 1)

            def attend(u):
                pe.wait_ge(v_copied, u + 1)
                pe.wait_ge(prob_t_done, JB * (u + 1))
                pe.wait_ge(exp_done, SUB * (u + 1))
                for t in range(SUB):
                    mm = nc.tensor.matmul(ps_o[:, t * P:(t + 1) * P], v_sb[:, u % 2, t, :],
                                          prob_t[:, t, :], start=True, stop=True)
                mm.then_inc(pv_done, 1)

            def project_out(u, t):
                if u == 0 and t == 0:
                    pe.wait_ge(wo_hi_done, 1)
                    pe.wait_ge(wo_lo_done, 1)
                if t == 0:
                    pe.wait_ge(o_hi_done, u + 1)
                    pe.wait_ge(o_lo_done, u + 1)
                if t == 0 and u > 0:
                    pe.wait_ge(gate_exp_done, SUB * u)
                if t > 0 and u < UNITS - 1:
                    pe.wait_ge(x2_done, SUB * u + t)
                if t > 0 and u == UNITS - 1:
                    pe.wait_ge(k_copied, UNITS)
                tok = slice(t * P, (t + 1) * P)
                for n, (o, w) in enumerate(((o_hi, wo_hi), (o_hi, wo_lo), (o_lo, wo_hi))):
                    mm = nc.tensor.matmul(wo_bank(u, t), o[:, tok], w[:], start=(n == 0), stop=(n == 2))
                mm.then_inc(wo_done, 1)

            def convolve(u):
                if u == 0:
                    pe.wait_ge(band_done, 1)
                pe.wait_ge(ysum_done, SUB * (u + 1))
                nc.tensor.matmul(ps_conv, band[:], ysum[:], start=True, stop=True) \
                    .then_inc(conv_done, 1)

            def transpose(v, t):
                if v == 0:
                    pe.wait_ge(ident_done, 1)
                pe.wait_ge(xq_done, SUB * v + t + 1)
                if v == STEPS - 1 and t == 1:
                    pe.wait_ge(v_copied, UNITS)
                elif v >= 1 and t == 0:
                    pe.wait_ge(xq_t_done, SUB * v)
                for c in range(TC):
                    mm = nc.tensor.transpose(turned(v, t, t + 1)[:, c, :],
                                             xq[:, v % 2, t, c * P:(c + 1) * P], ident[:])
                mm.then_inc(tr_done, 1)

            def ffn(u, t):
                if u == 0 and t == 0:
                    pe.wait_ge(bias_done, len(PART_ROWS))
                    pe.wait_ge(ones_done, 1)
                pe.wait_ge(xq_t_done, SUB * (WBLOCKS + u) + t + 1)
                bank = ffn_bank(u, t)
                if u >= UNITS - 2 and t > 0:
                    pe.wait_ge(mix_f_done, TILES)
                elif u == UNITS - 1:
                    pe.wait_ge(ffn_out_done, SUB * u - 1)
                elif u > 0 or t > 0:
                    pe.wait_ge(ffn_out_done, SUB * u + t)
                nc.tensor.matmul(bank, ones[:], bias_rows[:], start=True, stop=False)
                for c in range(TC):
                    mm = nc.tensor.matmul(bank, xq_t[:, u % 2, c, t * P:(t + 1) * P],
                                          wq_t[:, c, :], start=False, stop=(c == TC - 1))
                mm.then_inc(ffn_done, 1)

            mix(0)
            project_qk(0, 0)
            project_qk(0, 1)
            mix(1)
            scores(0)
            project_v(0)
            for s in range(STEPS):
                for t in range(SUB):
                    transpose(s, t)
                if is_unit(s + 1):
                    project_qk(s + 1, 0, 0, 1)
                if is_unit(s):
                    turn_v(s)
                if is_unit(s + 1):
                    project_qk(s + 1, 0, 1, 3)
                if is_unit(s):
                    attend(s)
                if is_unit(s + 2):
                    mix(s + 2)
                if is_unit(s):
                    project_out(s, 0)
                if is_unit(s + 1):
                    project_qk(s + 1, 1)
                if is_unit(s):
                    project_out(s, 1)
                if is_unit(s - 2):
                    ffn(s - 2, 0)
                if is_unit(s + 1):
                    scores(s + 1)
                    project_v(s + 1)
                if is_unit(s):
                    convolve(s)
                if is_unit(s - 2):
                    ffn(s - 2, 1)

        @block.scalar
        def _(act):
            nc.scalar.dma_start(wqkv_f[:], wqkv.rearrange("(c p) f -> p c f", p=P)) \
                .then_inc(wqkv_loaded, 16)
            nc.scalar.dma_start(ffn_w_f[:, 0:SUB], ffn_w[0:TOK].rearrange("(n p) t -> p n t", p=P)) \
                .then_inc(ffn_w_loaded[0], 16)
            nc.scalar.dma_start(bqkv_sb[:], bqkv.rearrange("(k d) -> d k", d=D),
                                allow_slow_non_contiguous=True).then_inc(bqkv_loaded, 16)

            def late_loads():
                nc.scalar.dma_start(bias_row[:], ffn_b.partition_broadcast(P)) \
                    .then_inc(bias_loaded, 16)
                nc.scalar.dma_start(bo_row[:, 0, :], bo.partition_broadcast(P)) \
                    .then_inc(bo_loaded, 16)
                nc.scalar.dma_start(wo_f[:], wo).then_inc(wo_loaded, 16)
                nc.scalar.dma_start(ffn_w_f[:, SUB:2 * SUB],
                                    ffn_w[TOK:2 * TOK].rearrange("(n p) t -> p n t", p=P)) \
                    .then_inc(ffn_w_loaded[1], 16)

            def split_weights():
                act.wait_ge(wqkv_loaded, 16)
                nc.scalar.activation(wqkv_hi[:], wqkv_f[:], ACT.Copy).then_inc(wqkv_hi_done, 1)
                act.wait_ge(bqkv_loaded, 16)
                nc.scalar.mul(bq_scaled[:], bqkv_sb[:, 0:1], QSCALE).then_inc(bq_done, 1)

            def split_wo():
                act.wait_ge(wo_loaded, 16)
                nc.scalar.activation(wo_hi[:], wo_f[:], ACT.Copy).then_inc(wo_hi_done, 1)

            def exp_scores(u):
                act.wait_ge(negmax_done, u + 1)
                if u >= 1:
                    act.wait_ge(prob_n_done, u)
                for t in range(SUB):
                    nc.scalar.activation(prob[:, t, :], ps_s[:, t, :], ACT.Exp,
                                         bias=negmax[:, t:t + 1],
                                         accum_out=psum_row[:, t:t + 1]).then_inc(exp_done, 1)

            def copy_mix(u):
                if u >= 2:
                    act.wait_ge(v_done, u - 1)
                    act.wait_ge(xc_lo_done, SUB * (u - 1))
                for t in range(SUB):
                    act.wait_ge(mix_done, SUB * u + t + 1)
                    tok = slice(t * P, (t + 1) * P)
                    nc.scalar.activation(xc_hi[:, u % 2, :, tok], ps_mix[t][:], ACT.Copy) \
                        .then_inc(xc_hi_done, 1)
                    nc.scalar.activation(mix_f[:, u % 2, :, tok], ps_mix[t][:], ACT.Copy) \
                        .then_inc(mix_f_done, 1)

            def magnitude(v, t):
                if v >= 2:
                    act.wait_ge(h_round_done, SUB * (v - 1))
                act.wait_ge(h_done, SUB * v + t + 1)
                nc.scalar.activation(h_mag[:, v % 2, t, :], h[:, v % 2, t, :], ACT.Abs,
                                     scale=ROUND_GAIN).then_inc(h_mag_done, 1)

            def copy_o_hi(u):
                act.wait_ge(pv_done, u + 1)
                if u >= 1:
                    act.wait_ge(wo_done, SUB * u)
                nc.scalar.activation(o_hi[:], ps_o, ACT.Copy).then_inc(o_hi_done, 1)

            def copy_qk(u):
                act.wait_ge(qk_done, u + 1)
                if u == 0:
                    act.wait_ge(bq_done, 1)
                if u >= 2:
                    act.wait_ge(scores_done, u - 1)
                nc.scalar.activation(q_t[:, u % 2], ps_qk[:, 0, :], ACT.Identity,
                                     bias=bq_scaled[:], scale=QSCALE).then_inc(q_copied, 1)
                nc.scalar.activation(k_t[:, u % 2], ps_qk[:, 1, :], ACT.Identity,
                                     bias=bqkv_sb[:, 1:2]).then_inc(k_copied, 1)

            def copy_v_t(u):
                act.wait_ge(v_done, u + 1)
                if u >= 1:
                    act.wait_ge(v_turned, u)
                nc.scalar.activation(v_t[:], ps_v[:], ACT.Identity, bias=bqkv_sb[:, 2:3]) \
                    .then_inc(v_t_copied, 1)

            def copy_v(u):
                act.wait_ge(v_turned, u + 1)
                if u >= 2:
                    act.wait_ge(pv_done, u - 1)
                nc.scalar.activation(v_sb[:, u % 2], ps_v[:].rearrange("p (t d) -> p t d", t=SUB),
                                     ACT.Copy).then_inc(v_copied, 1)

            def exp_gate(u):
                act.wait_ge(conv_done, u + 1)
                if u == 0:
                    act.wait_ge(neg_len_done, 1)
                if u >= 2:
                    act.wait_ge(gate_den_done, u - 1)
                for t in range(SUB):
                    i = SUB * u + t
                    nc.scalar.activation(eg[:, u % 2, t:t + 1], ps_conv[:, t:t + 1], ACT.Exp,
                                         scale=neg_len_inv[:, i:i + 1]).then_inc(gate_exp_done, 1)

            def copy_transposed(v, t0=0, t1=SUB):
                act.wait_ge(tr_done, SUB * v + t1)
                if v >= WBLOCKS + 2:
                    act.wait_ge(ffn_done, SUB * (v - WBLOCKS - 1))
                dst = wq_t[:, :, v * TOK:(v + 1) * TOK] if v < WBLOCKS else xq_t[:, v % 2]
                cols = slice(t0 * P, t1 * P)
                nc.scalar.activation(dst[:, :, cols], turned(v, t0, t1), ACT.Copy) \
                    .then_inc(xq_t_done, t1 - t0)

            def copy_ffn(u, t):
                act.wait_ge(ffn_done, SUB * u + t + 1)
                if u >= 1:
                    wait_result(act, u - 1, t)
                nc.scalar.activation(ffn_out[:, t, :], ffn_bank(u, t), ACT.Copy).then_inc(ffn_out_done, 1)

            split_weights()
            late_loads()
            copy_mix(0)
            magnitude(0, 0)
            magnitude(0, 1)
            split_wo()
            copy_qk(0)
            copy_mix(1)
            exp_scores(0)
            copy_v_t(0)
            for s in range(STEPS):
                if is_unit(s):
                    copy_v(s)
                if s == STEPS - 2:
                    copy_transposed(s)
                if s + 1 < STEPS:
                    magnitude(s + 1, 0)
                if is_unit(s):
                    copy_o_hi(s)
                if s + 1 < STEPS:
                    magnitude(s + 1, 1)
                if s + 1 < STEPS - 1:
                    copy_transposed(s)
                elif s == STEPS - 2:
                    pass
                else:
                    copy_transposed(s, 0, 1)
                    copy_transposed(s, 1, 2)
                if is_unit(s + 2):
                    copy_mix(s + 2)
                if is_unit(s + 1):
                    copy_qk(s + 1)
                if is_unit(s - 2):
                    copy_ffn(s - 2, 0)
                if is_unit(s + 1):
                    exp_scores(s + 1)
                    copy_v_t(s + 1)
                if is_unit(s):
                    exp_gate(s)
                if is_unit(s - 2):
                    copy_ffn(s - 2, 1)

        @block.vector
        def _(dve):
            def iotas():
                dve.wait_ge(iota_done, 2)
                nc.vector.tensor_copy(pos_f[:], pos_i[:]).then_inc(iota_f_done, 1)
                nc.vector.tensor_copy(diag_f[:], diag_i[:]).then_inc(iota_f_done, 1)
                dve.wait_ge(iota_f_done, 2)
                nc.vector.tensor_scalar(ident[:], diag_f[:], float(TAPS // 2), None, ALU.is_equal) \
                    .then_inc(ident_done, 1)
                nc.vector.tensor_scalar(ident_f[:], diag_f[:], float(TAPS // 2), None,
                                        ALU.is_equal).then_inc(ident_done, 1)

            def lengths():
                dve.wait_ge(len_loaded, 16)
                for j in range(JB):
                    p = slice(j * C, (j + 1) * C)
                    nc.vector.tensor_copy(len_f[p, :],
                                          len_i[p, :].rearrange("p (i j) -> p i j", j=JB)[:, :, j]) \
                        .then_inc(len_f_done, 1)
                dve.wait_ge(len_f_done, JB)
                nc.vector.reciprocal(len_inv[:], len_f[:]).then_inc(len_inv_done, 1)
                dve.wait_ge(len_inv_done, 1)
                nc.vector.tensor_scalar(neg_len_inv[:], len_inv[:], -1.0, None, ALU.mult) \
                    .then_inc(neg_len_done, 1)

            def band_matrix():
                nc.vector.memset(same[:], 0.0).then_inc(same_zeroed, 1)
                dve.wait_ge(same_zeroed, 1)
                for j in range(JB):
                    p = slice(j * C, (j + 1) * C)
                    nc.vector.memset(same[p, p], 1.0).then_inc(same_done, 1)
                dve.wait_ge(taps_loaded, 16)
                for k in range(TAPS):
                    nc.vector.tensor_scalar(band_k[:, k, :], diag_f[:], float(k), taps[:, k:k + 1],
                                            ALU.is_equal, ALU.mult).then_inc(band_parts, 1)
                dve.wait_ge(band_parts, TAPS)
                dve.wait_ge(same_done, JB)
                for k in range(1, TAPS):
                    if k >= 2:
                        dve.wait_ge(band_sums, k - 1)
                    nc.vector.tensor_tensor(band_k[:, 0, :], band_k[:, 0, :], band_k[:, k, :],
                                            ALU.add).then_inc(band_sums, 1)
                dve.wait_ge(band_sums, TAPS - 1)
                nc.vector.tensor_tensor(band[:], band_k[:, 0, :], same[:], ALU.mult) \
                    .then_inc(band_done, 1)

            def split_bias():
                dve.wait_ge(bias_loaded, 16)
                dve.wait_ge(bias_rows_zeroed, 1)
                rest = bias_row
                n = 0
                for k, row in enumerate(PART_ROWS):
                    if k < 2:
                        nc.vector.tensor_copy(bias_part[:, k, :], rest[:]).then_inc(bias_chain, 1)
                        n += 1
                        dve.wait_ge(bias_chain, n)
                        nc.vector.tensor_tensor(bias_rest[:, k, :], rest[:], bias_part[:, k, :],
                                                ALU.subtract).then_inc(bias_chain, 1)
                        n += 1
                        nc.vector.tensor_copy(bias_rows[row:row + 1, :],
                                              bias_part[row:row + 1, k, :]).then_inc(bias_done, 1)
                        dve.wait_ge(bias_chain, n)
                        rest = bias_rest[:, k, :]
                    else:
                        nc.vector.tensor_copy(bias_rows[row:row + 1, :], rest[row:row + 1, :]) \
                            .then_inc(bias_done, 1)

            def score_max(u):
                dve.wait_ge(scores_done, u + 1)
                if u >= 1:
                    dve.wait_ge(exp_done, SUB * u)
                nc.vector.tensor_reduce(negmax[:], ps_s, AX.X, ALU.max, negate=True) \
                    .then_inc(negmax_done, 1)

            def softmax_inverse(u):
                dve.wait_ge(exp_done, SUB * (u + 1))
                nc.vector.reciprocal(prob_inv[:], psum_row[:]).then_inc(prob_inv_done, 1)

            def softmax_divide(u):
                dve.wait_ge(prob_inv_done, u + 1)
                nc.vector.tensor_tensor(prob_n[:], prob[:],
                                        prob_inv[:].unsqueeze(2).to_broadcast([P, SUB, C]),
                                        ALU.mult).then_inc(prob_n_done, 1)

            def softmax_turn(u, j):
                if j == 0:
                    dve.wait_ge(prob_n_done, u + 1)
                    if u == 0:
                        dve.wait_ge(prob_t_zeroed, 1)
                    else:
                        dve.wait_ge(pv_done, u)
                p = slice(j * C, (j + 1) * C)
                nc.vector.transpose(prob_t[p, :, p], prob_n[p]).then_inc(prob_t_done, 1)

            def copy_o_lo(u):
                dve.wait_ge(o_hi_done, u + 1)
                nc.vector.tensor_tensor(o_lo[:], ps_o, o_hi[:].bitcast(F32), ALU.subtract) \
                    .then_inc(o_lo_done, 1)

            def residual_sum(u, t):
                if t == 0:
                    dve.wait_ge(xb_done, u + 1)
                if u >= 3:
                    dve.wait_ge(result_done, SUB * (u - 3) + t + 1)
                dve.wait_ge(wo_done, SUB * u + t + 1)
                nc.vector.tensor_tensor(x2[:, u % 3, t, :], wo_bank(u, t), xb[:, u % 2, t, :],
                                        ALU.add).then_inc(x2_done, 1)

            def masked_sum(u, t):
                i = SUB * u + t
                if u >= 1 and t == 0:
                    dve.wait_ge(conv_done, u)
                dve.wait_ge(x2_done, i + 1)
                nc.vector.scalar_tensor_tensor(out=masked[:, t, :], in0=pos_f[:],
                                               scalar=len_f[:, i:i + 1], in1=x2[:, u % 3, t, :],
                                               op0=ALU.is_lt, op1=ALU.mult,
                                               accum_out=ysum[:, t:t + 1]) \
                    .then_inc(ysum_done, 1)

            def block_max(v, t):
                if v < WBLOCKS:
                    dve.wait_ge(ffn_w_loaded[v], 16)
                    src = ffn_w_f[:, SUB * v:SUB * (v + 1)]
                else:
                    dve.wait_ge(x2_done, SUB * (v - WBLOCKS) + t + 1)
                    src = x2[:, (v - WBLOCKS) % 3]
                nc.vector.tensor_reduce(amax[:, v % 2, t, :],
                                        src[:, t, :].rearrange("p (n k) -> p n k", k=BLOCK),
                                        AX.X, ALU.max, apply_absolute_value=True) \
                    .then_inc(amax_done, 1)

            def gate_denominator(v):
                u = v - WBLOCKS
                dve.wait_ge(gate_exp_done, SUB * (u + 1))
                nc.vector.tensor_scalar(gate_den[:], eg[:, u % 2], 1.0, None, ALU.add) \
                    .then_inc(gate_den_done, 1)

            def gate_value(v):
                dve.wait_ge(gate_den_done, v - WBLOCKS + 1)
                nc.vector.reciprocal(gate[:], gate_den[:]).then_inc(gate_done, 1)

            def gated_max(v):
                dve.wait_ge(gate_done, v - WBLOCKS + 1)
                dve.wait_ge(amax_done, SUB * (v + 1))
                nc.vector.tensor_tensor(amax_g[:], amax[:, v % 2],
                                        gate[:].unsqueeze(2).to_broadcast([P, SUB, NB]), ALU.mult) \
                    .then_inc(amax_g_done, 1)

            def scale_exponent(v):
                if v < WBLOCKS:
                    top = amax[:, v % 2]
                    dve.wait_ge(amax_done, SUB * (v + 1))
                else:
                    top = amax_g[:]
                    dve.wait_ge(amax_g_done, v - WBLOCKS + 1)
                nc.vector.tensor_scalar(amax_e[:].bitcast(U32), top.bitcast(U32), EXP_MASK, None,
                                        ALU.bitwise_and).then_inc(amax_e_done, 1)

            def scale_value(v):
                dve.wait_ge(amax_e_done, v + 1)
                if v >= 2:
                    dve.wait_ge(xq_done, SUB * (v - 1))
                nc.vector.tensor_scalar(scale[:, v % 2], amax_e[:], AMAX_FLOOR,
                                        2.0 ** -E4M3_EMAX, ALU.max, ALU.mult) \
                    .then_inc(scale_done, 1)

            def scale_inverse(v):
                dve.wait_ge(scale_done, v + 1)
                nc.vector.tensor_scalar(inv[:].bitcast(I32), scale[:, v % 2].bitcast(I32), -1.0,
                                        float(254 * MANTISSA), ALU.mult, ALU.add) \
                    .then_inc(inv_done, 1)

            def gated_inverse(v):
                dve.wait_ge(inv_done, v + 1)
                nc.vector.tensor_tensor(inv_g[:], inv[:],
                                        gate[:].unsqueeze(2).to_broadcast([P, SUB, NB]), ALU.mult) \
                    .then_inc(inv_g_done, 1)

            def scaled(v):
                src = ffn_w_f[:, SUB * v:SUB * (v + 1)] if v < WBLOCKS else x2[:, (v - WBLOCKS) % 3]
                by = inv if v < WBLOCKS else inv_g
                if v < WBLOCKS:
                    dve.wait_ge(inv_done, v + 1)
                else:
                    dve.wait_ge(inv_g_done, v - WBLOCKS + 1)
                for t in range(SUB):
                    nc.vector.tensor_tensor(
                        h[:, v % 2, t, :].rearrange("p (n k) -> p n k", k=BLOCK),
                        src[:, t, :].rearrange("p (n k) -> p n k", k=BLOCK),
                        by[:, t, :].unsqueeze(2).to_broadcast([P, NB, BLOCK]), ALU.mult) \
                        .then_inc(h_done, 1)

            def round_sum(v, t):
                dve.wait_ge(h_mag_done, SUB * v + t + 1)
                nc.vector.scalar_tensor_tensor(out=h_sum[:, t, :], in0=h_mag[:, v % 2, t, :],
                                               scalar=ROUND_FLOOR, in1=h[:, v % 2, t, :],
                                               op0=ALU.max, op1=ALU.add) \
                    .then_inc(h_sum_done, 1)

            def round_back(v, t0=0, t1=SUB):
                dve.wait_ge(h_sum_done, SUB * v + t1)
                nc.vector.scalar_tensor_tensor(out=h_round[:, t0:t1], in0=h_mag[:, v % 2, t0:t1],
                                               scalar=ROUND_FLOOR, in1=h_sum[:, t0:t1],
                                               op0=ALU.max, op1=ALU.subtract) \
                    .then_inc(h_round_done, t1 - t0)

            def clip(v, t0=0, t1=SUB):
                dve.wait_ge(h_round_done, SUB * v + t1)
                if v >= 2:
                    dve.wait_ge(xq_done, SUB * (v - 1))
                nc.vector.tensor_scalar(h_clip[:, v % 2, t0:t1], h_round[:, t0:t1], E4M3_MAX,
                                        -E4M3_MAX, ALU.min, ALU.max) \
                    .then_inc(h_clip_done, t1 - t0)

            nc.vector.memset(mix_w[:], 0.0).then_inc(mix_w_zeroed, 1)
            iotas()
            lengths()

            block_max(0, 0)
            block_max(0, 1)
            scale_exponent(0)
            scale_value(0)
            scale_inverse(0)
            scaled(0)
            band_matrix()
            round_sum(0, 0)
            round_sum(0, 1)
            round_back(0)
            clip(0)
            block_max(1, 0)
            block_max(1, 1)
            split_bias()
            score_max(0)
            for s in range(STEPS):
                attends, quantises = is_unit(s), s + 1 < STEPS
                gates = quantises and s + 1 >= WBLOCKS
                if attends:
                    softmax_inverse(s)
                if gates:
                    gate_denominator(s + 1)
                if gates:
                    gate_value(s + 1)
                if attends:
                    softmax_divide(s)
                if gates:
                    gated_max(s + 1)
                if attends:
                    softmax_turn(s, 0)
                if quantises:
                    scale_exponent(s + 1)
                if attends:
                    softmax_turn(s, 1)
                if quantises:
                    scale_value(s + 1)
                if attends:
                    softmax_turn(s, 2)
                if quantises:
                    scale_inverse(s + 1)
                if attends:
                    softmax_turn(s, 3)
                if gates:
                    gated_inverse(s + 1)
                if quantises:
                    scaled(s + 1)
                    round_sum(s + 1, 0)
                if attends:
                    copy_o_lo(s)
                if quantises:
                    round_sum(s + 1, 1)
                if s + 1 < STEPS - 1:
                    round_back(s + 1)
                elif s == STEPS - 2:
                    for t in range(SUB):
                        round_back(s + 1, t, t + 1)
                        clip(s + 1, t, t + 1)
                if attends:
                    residual_sum(s, 0)
                if s + 1 < STEPS - 1:
                    clip(s + 1)
                if s == UNITS - 1:
                    residual_sum(s, 1)
                    masked_sum(s, 0)
                    masked_sum(s, 1)
                    block_max(s + WBLOCKS, 0)
                elif attends:
                    masked_sum(s, 0)
                    residual_sum(s, 1)
                    block_max(s + WBLOCKS, 0)
                if is_unit(s + 1):
                    score_max(s + 1)
                if s < UNITS - 1:
                    masked_sum(s, 1)
                if attends:
                    block_max(s + WBLOCKS, 1)
            for u in (UNITS - 2, UNITS - 1):
                for t in range(SUB):
                    final_sum(nc.vector, u, t)


_INS = ['x', 'itok_B_0_15', 'itok_B_9_3973', 'L0_cond_weights', 'L0_attn_Wqkv', 'L0_attn_bqkv', 'L0_attn_Wo',
        'L0_attn_bo', 'L0_cond2_conv_w', 'L0_ffn_weight', 'L0_ffn_bias']
_OUTS = [((64, 32, 512), 'float32')]


def kernel(**inputs):
    import numpy as _np
    import concourse.bacc as _bacc
    from concourse import mybir as _mybir
    from concourse.bass_utils import run_bass_kernel_spmd as _run

    nc = _bacc.Bacc("TRN2", target_bir_lowering=False, num_devices=1)
    arrays, args = {}, []
    for name in _INS:
        a = _np.ascontiguousarray(inputs[name])
        arrays[f"in_{name}_dram"] = a
        args.append(nc.dram_tensor(f"in_{name}_dram", a.shape, _mybir.dt.from_np(a.dtype), kind="ExternalInput").ap())
    for i, (shape, dtype) in enumerate(_OUTS):
        dt = _mybir.dt.from_np(_np.dtype(dtype))
        args.append(nc.dram_tensor(f"out_{i}_dram", shape, dt, kind="ExternalOutput").ap())
    adaln_attn_ffn_kernel(nc, *args)
    r = _run(nc, [arrays], core_ids=[0])
    got = tuple(r.results[0][f"out_{i}_dram"] for i in range(len(_OUTS)))
    return got[0]
```

```python
from contextlib import ExitStack

import concourse.bass as bass
from concourse import mybir

ALU = mybir.AluOpType
ACT = mybir.ActivationFunctionType
AX = mybir.AxisListType
F32 = mybir.dt.float32
F32R = mybir.dt.float32r
BF16 = mybir.dt.bfloat16
I32 = mybir.dt.int32
U32 = mybir.dt.uint32

P = 128
WARM_START = 26
SUB = 2
PART_ROWS = (0, 32, 64)
AHEAD = 5

BLOCK = 32
E4M3_MAX = 448.0
E4M3_EMAX = 8
ROUND_GAIN = float(2 ** 20)
ROUND_FLOOR = 1.5 * 2.0 ** -6 * ROUND_GAIN
EXP_MASK = 0x7F800000
MANTISSA = 1 << 23
AMAX_FLOOR = 2.0 ** (E4M3_EMAX - 126)


def adaln_attn_ffn_kernel(
    nc: bass.Bass,
    x: bass.AP,
    condition: bass.AP,
    length: bass.AP,
    cond_w: bass.AP,
    wqkv: bass.AP,
    bqkv: bass.AP,
    wo: bass.AP,
    bo: bass.AP,
    conv_w: bass.AP,
    ffn_w: bass.AP,
    ffn_b: bass.AP,
    out: bass.AP,
):
    B, C, T = x.shape
    D = wo.shape[0]
    N = ffn_w.shape[0]
    TAPS = conv_w.shape[2]
    JB = P // C
    TILES = B * C // P
    UNITS = TILES // SUB
    TC = T // P
    NB = T // BLOCK
    TOK = SUB * P
    WBLOCKS = N // TOK
    STEPS = UNITS + WBLOCKS
    QSCALE = float(D) ** -0.5
    assert C == 32 and T == 512 and N == 512 and D == P and WBLOCKS == 2

    x_v = x.rearrange("(i j) c t -> i (j c) t", j=JB)
    out_v = out.rearrange("(i j) c t -> i (j c) t", j=JB)

    with ExitStack() as ctx:
        def sb(name, shape, dt):
            return ctx.enter_context(nc.sbuf_tensor(name, shape, dt))

        def pb(name, shape, dt):
            return ctx.enter_context(nc.psum_tensor(name, shape, dt))

        def sem(name):
            return ctx.enter_context(nc.semaphore(name))

        wqkv_f = sb("wqkv_f", [P, TC, 3 * D], F32)
        wqkv_hi = sb("wqkv_hi", [P, TC, 3 * D], F32R)
        wqkv_lo = sb("wqkv_lo", [P, TC, 3 * D], F32R)
        wo_f = sb("wo_f", [P, T], F32)
        wo_hi = sb("wo_hi", [P, T], F32R)
        wo_lo = sb("wo_lo", [P, T], F32R)
        ffn_w_f = sb("ffn_w_f", [P, N // P, T], F32)
        wq_t = sb("wq_t", [P, TC, N], BF16)
        bqkv_sb = sb("bqkv_sb", [P, 3], F32)
        bq_scaled = sb("bq_scaled", [P, 1], F32)
        bo_row = sb("bo_row", [P, 1, T], F32)
        bias_row = sb("bias_row", [P, N], F32)
        bias_part = sb("bias_part", [P, 2, N], BF16)
        bias_rest = sb("bias_rest", [P, 2, N], F32)
        bias_rows = sb("bias_rows", [P, N], BF16)
        ones = sb("ones", [P, P], BF16)
        warm = sb("warm", [P, T], BF16)
        ident = sb("ident", [P, P], BF16)
        pos_i = sb("pos_i", [P, T], I32)
        pos_f = sb("pos_f", [P, T], F32)
        diag_i = sb("diag_i", [P, P], I32)
        diag_f = sb("diag_f", [P, P], F32)
        same = sb("same", [P, P], F32)
        taps = sb("taps", [P, TAPS], F32)
        band_k = sb("band_k", [P, TAPS, P], F32)
        band = sb("band", [P, P], F32)
        cond_row = sb("cond_row", [1, B], I32)
        len_i = sb("len_i", [P, B], I32)
        len_f = sb("len_f", [P, TILES], F32)
        len_inv = sb("len_inv", [P, TILES], F32)
        neg_len_inv = sb("neg_len_inv", [P, TILES], F32)

        x_sb = sb("x_sb", [P, UNITS, SUB, T], F32)
        mix_w = sb("mix_w", [P, UNITS, SUB, P], F32)

        mix_f = sb("mix_f", [P, 2, TC, TOK], F32)
        xc_hi = sb("xc_hi", [P, 2, TC, TOK], F32R)
        xc_lo = sb("xc_lo", [P, 2, TC, TOK], F32R)
        q_t = sb("q_t", [P, 2, TOK], F32)
        k_t = sb("k_t", [P, 2, TOK], F32)
        v_t = sb("v_t", [P, TOK], F32)
        v_sb = sb("v_sb", [P, 2, SUB, D], F32)
        ident_f = sb("ident_f", [P, P], F32)
        xb = sb("xb", [P, 2, SUB, T], F32)
        x2 = sb("x2", [P, 3, SUB, T], F32)
        eg = sb("eg", [P, 2, SUB], F32)
        negmax = sb("negmax", [P, SUB], F32)
        prob = sb("prob", [P, SUB, C], F32)
        psum_row = sb("psum_row", [P, SUB], F32)
        prob_inv = sb("prob_inv", [P, SUB], F32)
        prob_n = sb("prob_n", [P, SUB, C], F32)
        prob_t = sb("prob_t", [P, SUB, P], F32)
        o_hi = sb("o_hi", [P, TOK], F32R)
        o_lo = sb("o_lo", [P, TOK], F32R)
        masked = sb("masked", [P, SUB, T], F32)
        ysum = sb("ysum", [P, SUB], F32)
        gate_den = sb("gate_den", [P, SUB], F32)
        gate = sb("gate", [P, SUB], F32)
        amax = sb("amax", [P, 2, SUB, NB], F32)
        amax_g = sb("amax_g", [P, SUB, NB], F32)
        amax_e = sb("amax_e", [P, SUB, NB], F32)
        scale = sb("scale", [P, 2, SUB, NB], F32)
        inv = sb("inv", [P, SUB, NB], F32)
        inv_g = sb("inv_g", [P, SUB, NB], F32)
        h = sb("h", [P, 2, SUB, T], F32)
        h_mag = sb("h_mag", [P, 2, SUB, T], BF16)
        h_sum = sb("h_sum", [P, SUB, T], F32)
        h_round = sb("h_round", [P, SUB, T], BF16)
        h_clip = sb("h_clip", [P, 2, SUB, T], BF16)
        xq = sb("xq", [P, 2, SUB, T], BF16)
        xq_t = sb("xq_t", [P, 2, TC, TOK], BF16)
        ffn_out = sb("ffn_out", [P, SUB, N], BF16)
        result = sb("result", [P, SUB, T], F32)

        ps_mix = [pb(f"ps_mix{t}", [P, TC, P], F32) for t in range(SUB)]
        ps_qk = pb("ps_qk", [P, 2, TOK], F32)
        ps_v = pb("ps_v", [P, TOK], F32)
        ps_att = pb("ps_att", [P, 512], F32)
        ps_s = ps_att[:, 0:SUB * C].rearrange("p (t k) -> p t k", t=SUB)
        ps_o = ps_att[:, 0:TOK]
        ps_wo = pb("ps_wo", [P, T], F32)
        ps_conv = ps_wo[:, 0:SUB]
        ps_tr = pb("ps_tr", [P, TC, TOK], BF16)
        ps_ffn = pb("ps_ffn", [P, N], F32)

        x_loaded = [sem(f"x_loaded{u}") for u in range(UNITS)]
        cond_loaded = sem("cond_loaded")
        mix_w_loaded = [sem(f"mix_w_loaded{i}") for i in range(TILES)]
        wqkv_loaded = sem("wqkv_loaded")
        bqkv_loaded = sem("bqkv_loaded")
        wo_loaded = sem("wo_loaded")
        bo_loaded = sem("bo_loaded")
        ffn_w_loaded = [sem(f"ffn_w_loaded{v}") for v in range(WBLOCKS)]
        bias_loaded = sem("bias_loaded")
        taps_loaded = sem("taps_loaded")
        len_loaded = sem("len_loaded")
        stored = [sem(f"stored{t}") for t in range(SUB)]
        mix_w_zeroed = sem("mix_w_zeroed")
        warm_zeroed = sem("warm_zeroed")
        iota_done = sem("iota_done")
        iota_f_done = sem("iota_f_done")
        same_zeroed = sem("same_zeroed")
        same_done = sem("same_done")
        prob_t_zeroed = sem("prob_t_zeroed")
        ident_done = sem("ident_done")
        ones_done = sem("ones_done")
        band_parts = sem("band_parts")
        band_sums = sem("band_sums")
        band_done = sem("band_done")
        len_f_done = sem("len_f_done")
        len_inv_done = sem("len_inv_done")
        neg_len_done = sem("neg_len_done")
        wqkv_hi_done = sem("wqkv_hi_done")
        wqkv_lo_done = sem("wqkv_lo_done")
        wo_hi_done = sem("wo_hi_done")
        wo_lo_done = sem("wo_lo_done")
        bq_done = sem("bq_done")
        bias_part_done = sem("bias_part_done")
        bias_rest_done = sem("bias_rest_done")
        bias_done = sem("bias_done")
        bias_rows_zeroed = sem("bias_rows_zeroed")
        mix_done = sem("mix_done")
        xc_hi_done = sem("xc_hi_done")
        mix_f_done = sem("mix_f_done")
        xc_lo_done = sem("xc_lo_done")
        exp_done = sem("exp_done")
        wo_done = sem("wo_done")
        x2_done = sem("x2_done")
        ysum_done = sem("ysum_done")
        gate_exp_done = sem("gate_exp_done")
        ffn_done = sem("ffn_done")
        ffn_out_done = sem("ffn_out_done")
        result_done = sem("result_done")
        last_result_done = sem("last_result_done")
        qk_done = sem("qk_done")
        v_done = sem("v_done")
        q_copied = sem("q_copied")
        k_copied = sem("k_copied")
        v_t_copied = sem("v_t_copied")
        v_turned = sem("v_turned")
        v_copied = sem("v_copied")
        scores_done = sem("scores_done")
        negmax_done = sem("negmax_done")
        prob_inv_done = sem("prob_inv_done")
        prob_n_done = sem("prob_n_done")
        prob_t_done = sem("prob_t_done")
        pv_done = sem("pv_done")
        o_hi_done = sem("o_hi_done")
        o_lo_done = sem("o_lo_done")
        xb_done = sem("xb_done")
        conv_done = sem("conv_done")
        gate_den_done = sem("gate_den_done")
        gate_done = sem("gate_done")
        amax_g_done = sem("amax_g_done")
        inv_g_done = sem("inv_g_done")
        amax_e_done = sem("amax_e_done")
        scale_done = sem("scale_done")
        inv_done = sem("inv_done")
        amax_done = sem("amax_done")
        h_done = sem("h_done")
        h_mag_done = sem("h_mag_done")
        h_sum_done = sem("h_sum_done")
        h_round_done = sem("h_round_done")
        h_clip_done = sem("h_clip_done")
        xq_done = sem("xq_done")
        tr_done = sem("tr_done")
        xq_t_done = sem("xq_t_done")

        block = ctx.enter_context(nc.Block())

        def is_unit(u):
            return 0 <= u < UNITS

        def wo_bank(u, t):
            return ps_wo[:] if u < UNITS - 1 or t == 0 else ps_qk[:].rearrange("p k n -> p (k n)")

        def ffn_bank(u, t):
            return ps_ffn[:] if u < UNITS - 2 or t == 0 else \
                ps_mix[u - (UNITS - 2)][:].rearrange("p c k -> p (c k)")

        def turned(v, t0, t1):
            if v == STEPS - 1 and t0 == 1:
                return ps_v[:].bitcast(BF16).rearrange("p (c k) -> p c k", c=TC)
            return ps_tr[:, :, t0 * P:t1 * P]

        def wait_result(engine, u, t):
            if u < UNITS - 2:
                engine.wait_ge(result_done, SUB * u + t + 1)
            else:
                engine.wait_ge(last_result_done, SUB * (u - (UNITS - 2)) + t + 1)

        def final_sum(engine, u, t):
            engine.wait_ge(ffn_out_done, SUB * u + t + 1)
            engine.wait_ge(x2_done, SUB * u + t + 1)
            if u >= 1:
                engine.wait_ge(stored[t], 16 * u)
            engine.tensor_tensor(result[:, t, :], ffn_out[:, t, :], x2[:, u % 3, t, :],
                                 ALU.add) \
                .then_inc(result_done if u < UNITS - 2 else last_result_done, 1)

        def gather_mix_w(queue, u, t, batches=range(JB)):
            i = SUB * u + t
            for j in batches:
                b = i * JB + j
                k = queue.value_load(cond_row[0:1, b:b + 1], min_val=0,
                                     max_val=cond_w.shape[0] - 1)
                queue.dma_start(mix_w[C * j:C * (j + 1), u, t, C * j:C * (j + 1)],
                                cond_w[bass.ds(k, 1)].rearrange("k c d -> (k c) d")) \
                    .then_inc(mix_w_loaded[i], 16)

        @block.sync
        def _(sp):
            def load_x(u, t):
                nc.sync.dma_start(x_sb[:, u, t, :], x_v[SUB * u + t]).then_inc(x_loaded[u], 16)

            def store(u):
                for t in range(SUB):
                    wait_result(sp, u, t)
                    nc.sync.dma_start(out_v[SUB * u + t], result[:, t, :]) \
                        .then_inc(stored[t], 16)

            nc.sync.dma_start(cond_row[:], condition.rearrange("(a b) -> a b", a=1)) \
                .then_inc(cond_loaded, 16)
            load_x(0, 0)
            load_x(0, 1)
            sp.wait_ge(cond_loaded, 16)
            sp.wait_ge(mix_w_zeroed, 1)
            gather_mix_w(nc.sync, 0, 0)
            for u in range(1, UNITS):
                nc.sync.dma_start(x_sb[:, u],
                                  x_v[SUB * u:SUB * (u + 1)].rearrange("i p t -> p i t")) \
                    .then_inc(x_loaded[u], 32)
                for t in range(SUB if u > 1 else 1):
                    gather_mix_w(nc.sync, u, t)
                if u >= AHEAD:
                    store(u - AHEAD)
            for u in range(UNITS - AHEAD, UNITS):
                store(u)
            for t in range(SUB):
                sp.wait_ge(stored[t], 16 * UNITS)

        @block.gpsimd
        def _(pool):
            nc.gpsimd.dma_start(len_i[:], length.partition_broadcast(P)).then_inc(len_loaded, 16)
            nc.gpsimd.dma_start(taps[:],
                                conv_w.rearrange("a b k -> (a b k)").partition_broadcast(P)) \
                .then_inc(taps_loaded, 16)
            nc.gpsimd.iota(diag_i[:], [[-1, P]], base=TAPS // 2, channel_multiplier=1) \
                .then_inc(iota_done, 1)
            nc.gpsimd.iota(pos_i[:], [[1, T]], channel_multiplier=0).then_inc(iota_done, 1)
            pool.wait_ge(cond_loaded, 16)
            pool.wait_ge(mix_w_zeroed, 1)
            gather_mix_w(nc.gpsimd, 0, 1)
            nc.gpsimd.memset(bias_rows[:], 0.0).then_inc(bias_rows_zeroed, 1)
            nc.gpsimd.memset(prob_t[:], 0.0).then_inc(prob_t_zeroed, 1)
            nc.gpsimd.memset(ones[:], 1.0).then_inc(ones_done, 1)

            def residual(u):
                pool.wait_ge(x_loaded[u], 32)
                if u == 0:
                    pool.wait_ge(bo_loaded, 16)
                if u >= 2:
                    pool.wait_ge(x2_done, SUB * (u - 1))
                nc.gpsimd.tensor_tensor(xb[:, u % 2], x_sb[:, u],
                                        bo_row[:].to_broadcast([P, SUB, T]), ALU.add) \
                    .then_inc(xb_done, 1)

            def split_mix_lo(u, t):
                if u >= 2:
                    pool.wait_ge(v_done, u - 1)
                pool.wait_ge(mix_f_done, SUB * u + t + 1)
                tok = slice(t * P, (t + 1) * P)
                nc.gpsimd.tensor_tensor(xc_lo[:, u % 2, :, tok], mix_f[:, u % 2, :, tok],
                                        xc_hi[:, u % 2, :, tok].bitcast(F32), ALU.subtract) \
                    .then_inc(xc_lo_done, 1)

            def dequantise(v, t0=0, t1=SUB):
                pool.wait_ge(h_clip_done, SUB * v + t1)
                pool.wait_ge(scale_done, v + 1)
                if v >= 2:
                    pool.wait_ge(tr_done, SUB * (v - 1))
                nc.gpsimd.tensor_tensor(
                    xq[:, v % 2, t0:t1].rearrange("p t (n k) -> p (t n) k", k=BLOCK),
                    h_clip[:, v % 2, t0:t1].rearrange("p t (n k) -> p (t n) k", k=BLOCK),
                    scale[:, v % 2, t0:t1].rearrange("p t n -> p (t n)").unsqueeze(2)
                    .to_broadcast([P, (t1 - t0) * NB, BLOCK]), ALU.mult) \
                    .then_inc(xq_done, t1 - t0)

            def bias_low(k):
                pool.wait_ge(bias_part_done, k + 1)
                if k == 1:
                    pool.wait_ge(bias_rest_done, 1)
                rest = bias_row[:] if k == 0 else bias_rest[:, k - 1, :]
                nc.gpsimd.tensor_tensor(bias_rest[:, k, :], rest, bias_part[:, k, :],
                                        ALU.subtract).then_inc(bias_rest_done, 1)

            split_mix_lo(0, 0)
            split_mix_lo(0, 1)
            bias_low(0)
            split_mix_lo(1, 0)
            dequantise(0)
            split_mix_lo(1, 1)
            for s in range(UNITS - 1):
                residual(s)
                dequantise(s + 1)
                if is_unit(s + 2):
                    split_mix_lo(s + 2, 0)
                if s >= 2:
                    final_sum(nc.gpsimd, s - 2, 0)
                if is_unit(s + 2):
                    split_mix_lo(s + 2, 1)
                if s >= 2:
                    final_sum(nc.gpsimd, s - 2, 1)
                if s == 0:
                    bias_low(1)
            residual(UNITS - 1)
            final_sum(nc.gpsimd, UNITS - 3, 0)
            dequantise(UNITS)
            final_sum(nc.gpsimd, UNITS - 3, 1)
            dequantise(STEPS - 1, 0, 1)
            dequantise(STEPS - 1, 1, 2)

        @block.tensor
        def _(pe):
            pe.wait_ge(warm_zeroed, 1)

            def keep_warm(n):
                for _ in range(n):
                    nc.tensor.matmul(ps_att[:], warm[:, 0:P], warm[:], start=True, stop=True)

            def mix(u, t):
                pe.wait_ge(x_loaded[u], 32)
                pe.wait_ge(mix_w_loaded[SUB * u + t], 16 * JB)
                if u >= 1:
                    pe.wait_ge(mix_f_done, SUB * (u - 1) + t + 1)
                for c in range(TC):
                    mm = nc.tensor.matmul(ps_mix[t][:, c, :], x_sb[:, u, t, c * P:(c + 1) * P],
                                          mix_w[:, u, t, :], start=True, stop=True)
                mm.then_inc(mix_done, 1)

            def passes(u):
                hi, lo = xc_hi[:, u % 2], xc_lo[:, u % 2]
                return [(a, b, c) for a, b in ((wqkv_hi, hi), (wqkv_lo, hi), (wqkv_hi, lo))
                        for c in range(TC)]

            def project_qk(u, which, first=0, last=3):
                if which == 0 and first == 0:
                    if u == 0:
                        pe.wait_ge(wqkv_hi_done, 1)
                        pe.wait_ge(wqkv_lo_done, 1)
                    else:
                        pe.wait_ge(k_copied, u)
                    pe.wait_ge(xc_hi_done, SUB * (u + 1))
                steps = passes(u)
                for n in range(first * TC, last * TC):
                    w, xt, c = steps[n]
                    if n == 2 * TC and which == 0:
                        pe.wait_ge(xc_lo_done, SUB * (u + 1))
                    mm = nc.tensor.matmul(ps_qk[:, which, :], w[:, c, which * D:(which + 1) * D],
                                          xt[:, c, :], start=(n == 0), stop=(n == len(steps) - 1))
                if which == 1 and last == 3:
                    mm.then_inc(qk_done, 1)

            def project_v(u, first=0, last=3):
                if u >= 1:
                    pe.wait_ge(v_copied, u)
                steps = passes(u)
                for n in range(first * TC, last * TC):
                    w, xt, c = steps[n]
                    if n == 2 * TC:
                        pe.wait_ge(xc_lo_done, SUB * (u + 1))
                    mm = nc.tensor.matmul(ps_v[:], w[:, c, 2 * D:3 * D], xt[:, c, :],
                                          start=(n == 0), stop=(n == len(steps) - 1))
                if last == 3:
                    mm.then_inc(v_done, 1)

            def turn_v(u):
                if u == 0:
                    pe.wait_ge(ident_done, 2)
                pe.wait_ge(v_t_copied, u + 1)
                for t in range(SUB):
                    tok = slice(t * P, (t + 1) * P)
                    mm = nc.tensor.transpose(ps_v[:, tok], v_t[:, tok], ident_f[:])
                mm.then_inc(v_turned, 1)

            def scores(u):
                pe.wait_ge(q_copied, u + 1)
                pe.wait_ge(k_copied, u + 1)
                if u >= 1:
                    pe.wait_ge(o_hi_done, u)
                    pe.wait_ge(o_lo_done, u)
                for t in range(SUB):
                    for j in range(JB):
                        tok = slice(t * P + j * C, t * P + (j + 1) * C)
                        mm = nc.tensor.matmul(ps_s[j * C:(j + 1) * C, t, :], q_t[:, u % 2, tok],
                                              k_t[:, u % 2, tok], start=True, stop=True)
                mm.then_inc(scores_done, 1)

            def attend(u):
                pe.wait_ge(v_copied, u + 1)
                pe.wait_ge(prob_t_done, JB * (u + 1))
                pe.wait_ge(exp_done, SUB * (u + 1))
                for t in range(SUB):
                    mm = nc.tensor.matmul(ps_o[:, t * P:(t + 1) * P], v_sb[:, u % 2, t, :],
                                          prob_t[:, t, :], start=True, stop=True)
                mm.then_inc(pv_done, 1)

            def project_out(u, t):
                if u == 0 and t == 0:
                    pe.wait_ge(wo_hi_done, 1)
                    pe.wait_ge(wo_lo_done, 1)
                if t == 0:
                    pe.wait_ge(o_hi_done, u + 1)
                    pe.wait_ge(o_lo_done, u + 1)
                if t == 0 and u > 0:
                    pe.wait_ge(gate_exp_done, SUB * u)
                if t > 0 and u < UNITS - 1:
                    pe.wait_ge(x2_done, SUB * u + t)
                if t > 0 and u == UNITS - 1:
                    pe.wait_ge(k_copied, UNITS)
                tok = slice(t * P, (t + 1) * P)
                for n, (o, w) in enumerate(((o_hi, wo_hi), (o_hi, wo_lo), (o_lo, wo_hi))):
                    mm = nc.tensor.matmul(wo_bank(u, t), o[:, tok], w[:],
                                          start=(n == 0), stop=(n == 2))
                mm.then_inc(wo_done, 1)

            def convolve(u):
                if u == 0:
                    pe.wait_ge(band_done, 1)
                pe.wait_ge(ysum_done, SUB * (u + 1))
                nc.tensor.matmul(ps_conv, band[:], ysum[:], start=True, stop=True) \
                    .then_inc(conv_done, 1)

            def transpose(v, t):
                if v == 0:
                    pe.wait_ge(ident_done, 1)
                pe.wait_ge(xq_done, SUB * v + t + 1)
                if v == STEPS - 1 and t == 1:
                    pe.wait_ge(v_copied, UNITS)
                elif v >= 1 and t == 0:
                    pe.wait_ge(xq_t_done, SUB * v)
                for c in range(TC):
                    mm = nc.tensor.transpose(turned(v, t, t + 1)[:, c, :],
                                             xq[:, v % 2, t, c * P:(c + 1) * P], ident[:])
                mm.then_inc(tr_done, 1)

            def ffn(u, t):
                if u == 0 and t == 0:
                    pe.wait_ge(bias_done, len(PART_ROWS))
                    pe.wait_ge(ones_done, 1)
                pe.wait_ge(xq_t_done, SUB * (WBLOCKS + u) + t + 1)
                bank = ffn_bank(u, t)
                if u >= UNITS - 2 and t > 0:
                    pe.wait_ge(mix_f_done, TILES)
                elif u == UNITS - 1:
                    pe.wait_ge(ffn_out_done, SUB * u - 1)
                elif u > 0 or t > 0:
                    pe.wait_ge(ffn_out_done, SUB * u + t)
                nc.tensor.matmul(bank, ones[:], bias_rows[:], start=True, stop=False)
                for c in range(TC):
                    mm = nc.tensor.matmul(bank, xq_t[:, u % 2, c, t * P:(t + 1) * P],
                                          wq_t[:, c, :], start=False, stop=(c == TC - 1))
                mm.then_inc(ffn_done, 1)

            keep_warm(WARM_START)
            mix(0, 0)
            mix(0, 1)
            project_qk(0, 0, 0, 2)
            project_v(0, 0, 2)
            project_qk(0, 0, 2, 3)
            project_v(0, 2, 3)
            project_qk(0, 1)
            mix(1, 0)
            mix(1, 1)
            scores(0)
            for s in range(UNITS - 1):
                transpose(s, 0)
                transpose(s, 1)
                turn_v(s)
                project_qk(s + 1, 0)
                attend(s)
                if is_unit(s + 2):
                    mix(s + 2, 0)
                    mix(s + 2, 1)
                project_out(s, 0)
                project_qk(s + 1, 1)
                project_out(s, 1)
                scores(s + 1)
                if s >= 2:
                    ffn(s - 2, 0)
                project_v(s + 1)
                convolve(s)
                if s >= 2:
                    ffn(s - 2, 1)
            turn_v(UNITS - 1)
            transpose(UNITS - 1, 0)
            transpose(UNITS - 1, 1)
            attend(UNITS - 1)
            ffn(UNITS - 3, 0)
            project_out(UNITS - 1, 0)
            project_out(UNITS - 1, 1)
            convolve(UNITS - 1)
            ffn(UNITS - 3, 1)
            transpose(UNITS, 0)
            transpose(UNITS, 1)
            ffn(UNITS - 2, 0)
            ffn(UNITS - 2, 1)
            keep_warm(4)
            transpose(STEPS - 1, 0)
            transpose(STEPS - 1, 1)
            ffn(UNITS - 1, 0)
            ffn(UNITS - 1, 1)

        @block.scalar
        def _(act):
            nc.scalar.dma_start(wqkv_f[:], wqkv.rearrange("(c p) f -> p c f", p=P)) \
                .then_inc(wqkv_loaded, 16)
            nc.scalar.dma_start(ffn_w_f[:, 0:SUB], ffn_w[0:TOK].rearrange("(n p) t -> p n t", p=P)) \
                .then_inc(ffn_w_loaded[0], 16)
            nc.scalar.dma_start(bqkv_sb[:], bqkv.rearrange("(k d) -> d k", d=D),
                                allow_slow_non_contiguous=True).then_inc(bqkv_loaded, 16)

            def late_loads():
                nc.scalar.dma_start(bias_row[:], ffn_b.partition_broadcast(P)) \
                    .then_inc(bias_loaded, 16)
                nc.scalar.dma_start(bo_row[:, 0, :], bo.partition_broadcast(P)) \
                    .then_inc(bo_loaded, 16)
                nc.scalar.dma_start(wo_f[:], wo).then_inc(wo_loaded, 16)
                nc.scalar.dma_start(ffn_w_f[:, SUB:2 * SUB],
                                    ffn_w[TOK:2 * TOK].rearrange("(n p) t -> p n t", p=P)) \
                    .then_inc(ffn_w_loaded[1], 16)

            def split_wqkv_hi():
                act.wait_ge(wqkv_loaded, 16)
                nc.scalar.activation(wqkv_hi[:], wqkv_f[:], ACT.Copy).then_inc(wqkv_hi_done, 1)

            def gather_unit_1(batches):
                act.wait_ge(cond_loaded, 16)
                act.wait_ge(mix_w_zeroed, 1)
                gather_mix_w(nc.scalar, 1, 1, batches)

            def scale_bq():
                act.wait_ge(bqkv_loaded, 16)
                nc.scalar.mul(bq_scaled[:], bqkv_sb[:, 0:1], QSCALE).then_inc(bq_done, 1)

            def bias_high(k):
                if k == 0:
                    act.wait_ge(bias_loaded, 16)
                    act.wait_ge(bias_rows_zeroed, 1)
                else:
                    act.wait_ge(bias_rest_done, k)
                rest, row = (bias_row[:] if k == 0 else bias_rest[:, k - 1, :]), PART_ROWS[k]
                if k < 2:
                    nc.scalar.activation(bias_part[:, k, :], rest, ACT.Copy) \
                        .then_inc(bias_part_done, 1)
                nc.scalar.activation(bias_rows[row:row + 1, :], rest[row:row + 1, :], ACT.Copy) \
                    .then_inc(bias_done, 1)

            def split_wo_hi():
                act.wait_ge(wo_loaded, 16)
                nc.scalar.activation(wo_hi[:], wo_f[:], ACT.Copy).then_inc(wo_hi_done, 1)

            def exp_scores(u):
                act.wait_ge(negmax_done, u + 1)
                if u >= 1:
                    act.wait_ge(prob_n_done, u)
                for t in range(SUB):
                    nc.scalar.activation(prob[:, t, :], ps_s[:, t, :], ACT.Exp,
                                         bias=negmax[:, t:t + 1],
                                         accum_out=psum_row[:, t:t + 1]).then_inc(exp_done, 1)

            def copy_mix(u, t):
                if u >= 2:
                    act.wait_ge(v_done, u - 1)
                    act.wait_ge(xc_lo_done, SUB * (u - 1))
                act.wait_ge(mix_done, SUB * u + t + 1)
                tok = slice(t * P, (t + 1) * P)
                nc.scalar.activation(xc_hi[:, u % 2, :, tok], ps_mix[t][:], ACT.Copy) \
                    .then_inc(xc_hi_done, 1)
                nc.scalar.activation(mix_f[:, u % 2, :, tok], ps_mix[t][:], ACT.Copy) \
                    .then_inc(mix_f_done, 1)

            def magnitude(v, t):
                if v >= 2:
                    act.wait_ge(h_round_done, SUB * (v - 1))
                act.wait_ge(h_done, SUB * v + t + 1)
                nc.scalar.activation(h_mag[:, v % 2, t, :], h[:, v % 2, t, :], ACT.Abs,
                                     scale=ROUND_GAIN).then_inc(h_mag_done, 1)

            def copy_o_hi(u):
                act.wait_ge(pv_done, u + 1)
                if u >= 1:
                    act.wait_ge(wo_done, SUB * u)
                nc.scalar.activation(o_hi[:], ps_o, ACT.Copy).then_inc(o_hi_done, 1)

            def copy_qk(u):
                act.wait_ge(qk_done, u + 1)
                if u == 0:
                    act.wait_ge(bq_done, 1)
                if u >= 2:
                    act.wait_ge(scores_done, u - 1)
                nc.scalar.activation(q_t[:, u % 2], ps_qk[:, 0, :], ACT.Identity,
                                     bias=bq_scaled[:], scale=QSCALE).then_inc(q_copied, 1)
                nc.scalar.activation(k_t[:, u % 2], ps_qk[:, 1, :], ACT.Identity,
                                     bias=bqkv_sb[:, 1:2]).then_inc(k_copied, 1)

            def copy_v_t(u):
                act.wait_ge(v_done, u + 1)
                if u >= 1:
                    act.wait_ge(v_turned, u)
                nc.scalar.activation(v_t[:], ps_v[:], ACT.Identity, bias=bqkv_sb[:, 2:3]) \
                    .then_inc(v_t_copied, 1)

            def copy_v(u):
                act.wait_ge(v_turned, u + 1)
                if u >= 2:
                    act.wait_ge(pv_done, u - 1)
                nc.scalar.activation(v_sb[:, u % 2], ps_v[:].rearrange("p (t d) -> p t d", t=SUB),
                                     ACT.Copy).then_inc(v_copied, 1)

            def exp_gate(u):
                act.wait_ge(conv_done, u + 1)
                if u == 0:
                    act.wait_ge(neg_len_done, 1)
                if u >= 2:
                    act.wait_ge(gate_den_done, u - 1)
                for t in range(SUB):
                    i = SUB * u + t
                    nc.scalar.activation(eg[:, u % 2, t:t + 1], ps_conv[:, t:t + 1], ACT.Exp,
                                         scale=neg_len_inv[:, i:i + 1]).then_inc(gate_exp_done, 1)

            def copy_transposed(v, t0=0, t1=SUB):
                act.wait_ge(tr_done, SUB * v + t1)
                if v >= WBLOCKS + 2:
                    act.wait_ge(ffn_done, SUB * (v - WBLOCKS - 1))
                dst = wq_t[:, :, v * TOK:(v + 1) * TOK] if v < WBLOCKS else xq_t[:, v % 2]
                cols = slice(t0 * P, t1 * P)
                nc.scalar.activation(dst[:, :, cols], turned(v, t0, t1), ACT.Copy) \
                    .then_inc(xq_t_done, t1 - t0)

            def copy_ffn(u, t):
                act.wait_ge(ffn_done, SUB * u + t + 1)
                if u >= 1:
                    wait_result(act, u - 1, t)
                nc.scalar.activation(ffn_out[:, t, :], ffn_bank(u, t), ACT.Copy).then_inc(ffn_out_done, 1)

            split_wqkv_hi()
            gather_unit_1((0, 1))
            late_loads()
            copy_mix(0, 0)
            copy_mix(0, 1)
            split_wo_hi()
            magnitude(0, 0)
            magnitude(0, 1)
            gather_unit_1((2, 3))
            bias_high(0)
            scale_bq()
            copy_qk(0)
            copy_mix(1, 0)
            exp_scores(0)
            copy_mix(1, 1)
            copy_v_t(0)
            for s in range(UNITS - 1):
                copy_v(s)
                magnitude(s + 1, 0)
                copy_o_hi(s)
                magnitude(s + 1, 1)
                copy_transposed(s)
                if is_unit(s + 2):
                    copy_mix(s + 2, 0)
                copy_qk(s + 1)
                if is_unit(s + 2):
                    copy_mix(s + 2, 1)
                if s >= 2:
                    copy_ffn(s - 2, 0)
                exp_scores(s + 1)
                exp_gate(s)
                copy_v_t(s + 1)
                if s < 2:
                    bias_high(s + 1)
                if s >= 2:
                    copy_ffn(s - 2, 1)
            copy_v(UNITS - 1)
            copy_transposed(UNITS - 1)
            magnitude(UNITS, 0)
            copy_o_hi(UNITS - 1)
            magnitude(UNITS, 1)
            copy_ffn(UNITS - 3, 0)
            exp_gate(UNITS - 1)
            copy_ffn(UNITS - 3, 1)
            copy_transposed(UNITS)
            magnitude(STEPS - 1, 0)
            magnitude(STEPS - 1, 1)
            copy_ffn(UNITS - 2, 0)
            copy_ffn(UNITS - 2, 1)
            copy_transposed(STEPS - 1, 0, 1)
            copy_transposed(STEPS - 1, 1, 2)
            copy_ffn(UNITS - 1, 0)
            copy_ffn(UNITS - 1, 1)

        @block.vector
        def _(dve):
            def split_wqkv_lo():
                dve.wait_ge(wqkv_hi_done, 1)
                nc.vector.tensor_tensor(wqkv_lo[:], wqkv_f[:], wqkv_hi[:].bitcast(F32),
                                        ALU.subtract).then_inc(wqkv_lo_done, 1)

            def split_wo_lo():
                dve.wait_ge(wo_hi_done, 1)
                nc.vector.tensor_tensor(wo_lo[:], wo_f[:], wo_hi[:].bitcast(F32), ALU.subtract) \
                    .then_inc(wo_lo_done, 1)

            def iotas():
                dve.wait_ge(iota_done, 2)
                nc.vector.tensor_copy(pos_f[:], pos_i[:]).then_inc(iota_f_done, 1)
                nc.vector.tensor_copy(diag_f[:], diag_i[:]).then_inc(iota_f_done, 1)
                dve.wait_ge(iota_f_done, 2)
                nc.vector.tensor_scalar(ident[:], diag_f[:], float(TAPS // 2), None, ALU.is_equal) \
                    .then_inc(ident_done, 1)
                nc.vector.tensor_scalar(ident_f[:], diag_f[:], float(TAPS // 2), None,
                                        ALU.is_equal).then_inc(ident_done, 1)

            def lengths():
                dve.wait_ge(len_loaded, 16)
                for j in range(JB):
                    p = slice(j * C, (j + 1) * C)
                    nc.vector.tensor_copy(len_f[p, :],
                                          len_i[p, :].rearrange("p (i j) -> p i j", j=JB)[:, :, j]) \
                        .then_inc(len_f_done, 1)
                dve.wait_ge(len_f_done, JB)
                nc.vector.reciprocal(len_inv[:], len_f[:]).then_inc(len_inv_done, 1)
                dve.wait_ge(len_inv_done, 1)
                nc.vector.tensor_scalar(neg_len_inv[:], len_inv[:], -1.0, None, ALU.mult) \
                    .then_inc(neg_len_done, 1)

            def band_matrix():
                nc.vector.memset(same[:], 0.0).then_inc(same_zeroed, 1)
                dve.wait_ge(same_zeroed, 1)
                for j in range(JB):
                    p = slice(j * C, (j + 1) * C)
                    nc.vector.memset(same[p, p], 1.0).then_inc(same_done, 1)
                dve.wait_ge(taps_loaded, 16)
                for k in range(TAPS):
                    nc.vector.tensor_scalar(band_k[:, k, :], diag_f[:], float(k), taps[:, k:k + 1],
                                            ALU.is_equal, ALU.mult).then_inc(band_parts, 1)
                dve.wait_ge(band_parts, TAPS)
                dve.wait_ge(same_done, JB)
                for k in range(1, TAPS):
                    if k >= 2:
                        dve.wait_ge(band_sums, k - 1)
                    nc.vector.tensor_tensor(band_k[:, 0, :], band_k[:, 0, :], band_k[:, k, :],
                                            ALU.add).then_inc(band_sums, 1)
                dve.wait_ge(band_sums, TAPS - 1)
                nc.vector.tensor_tensor(band[:], band_k[:, 0, :], same[:], ALU.mult) \
                    .then_inc(band_done, 1)

            def score_max(u):
                dve.wait_ge(scores_done, u + 1)
                if u >= 1:
                    dve.wait_ge(exp_done, SUB * u)
                nc.vector.tensor_reduce(negmax[:], ps_s, AX.X, ALU.max, negate=True) \
                    .then_inc(negmax_done, 1)

            def softmax_inverse(u):
                dve.wait_ge(exp_done, SUB * (u + 1))
                nc.vector.reciprocal(prob_inv[:], psum_row[:]).then_inc(prob_inv_done, 1)

            def softmax_divide(u):
                dve.wait_ge(prob_inv_done, u + 1)
                nc.vector.tensor_tensor(prob_n[:], prob[:],
                                        prob_inv[:].unsqueeze(2).to_broadcast([P, SUB, C]),
                                        ALU.mult).then_inc(prob_n_done, 1)

            def softmax_turn(u, j):
                if j == 0:
                    dve.wait_ge(prob_n_done, u + 1)
                    if u == 0:
                        dve.wait_ge(prob_t_zeroed, 1)
                    else:
                        dve.wait_ge(pv_done, u)
                p = slice(j * C, (j + 1) * C)
                nc.vector.transpose(prob_t[p, :, p], prob_n[p]).then_inc(prob_t_done, 1)

            def copy_o_lo(u):
                dve.wait_ge(o_hi_done, u + 1)
                nc.vector.tensor_tensor(o_lo[:], ps_o, o_hi[:].bitcast(F32), ALU.subtract) \
                    .then_inc(o_lo_done, 1)

            def residual_sum(u, t):
                if t == 0:
                    dve.wait_ge(xb_done, u + 1)
                if u >= 3:
                    dve.wait_ge(result_done, SUB * (u - 3) + t + 1)
                dve.wait_ge(wo_done, SUB * u + t + 1)
                nc.vector.tensor_tensor(x2[:, u % 3, t, :], wo_bank(u, t), xb[:, u % 2, t, :],
                                        ALU.add).then_inc(x2_done, 1)

            def masked_sum(u, t):
                i = SUB * u + t
                if u >= 1 and t == 0:
                    dve.wait_ge(conv_done, u)
                dve.wait_ge(x2_done, i + 1)
                nc.vector.scalar_tensor_tensor(out=masked[:, t, :], in0=pos_f[:],
                                               scalar=len_f[:, i:i + 1], in1=x2[:, u % 3, t, :],
                                               op0=ALU.is_lt, op1=ALU.mult,
                                               accum_out=ysum[:, t:t + 1]) \
                    .then_inc(ysum_done, 1)

            def block_max(v, t):
                if v < WBLOCKS:
                    dve.wait_ge(ffn_w_loaded[v], 16)
                    src = ffn_w_f[:, SUB * v:SUB * (v + 1)]
                else:
                    dve.wait_ge(x2_done, SUB * (v - WBLOCKS) + t + 1)
                    src = x2[:, (v - WBLOCKS) % 3]
                nc.vector.tensor_reduce(amax[:, v % 2, t, :],
                                        src[:, t, :].rearrange("p (n k) -> p n k", k=BLOCK),
                                        AX.X, ALU.max, apply_absolute_value=True) \
                    .then_inc(amax_done, 1)

            def gate_denominator(v):
                u = v - WBLOCKS
                dve.wait_ge(gate_exp_done, SUB * (u + 1))
                nc.vector.tensor_scalar(gate_den[:], eg[:, u % 2], 1.0, None, ALU.add) \
                    .then_inc(gate_den_done, 1)

            def gate_value(v):
                dve.wait_ge(gate_den_done, v - WBLOCKS + 1)
                nc.vector.reciprocal(gate[:], gate_den[:]).then_inc(gate_done, 1)

            def gated_max(v):
                dve.wait_ge(gate_done, v - WBLOCKS + 1)
                dve.wait_ge(amax_done, SUB * (v + 1))
                nc.vector.tensor_tensor(amax_g[:], amax[:, v % 2],
                                        gate[:].unsqueeze(2).to_broadcast([P, SUB, NB]), ALU.mult) \
                    .then_inc(amax_g_done, 1)

            def scale_exponent(v):
                if v < WBLOCKS:
                    top = amax[:, v % 2]
                    dve.wait_ge(amax_done, SUB * (v + 1))
                else:
                    top = amax_g[:]
                    dve.wait_ge(amax_g_done, v - WBLOCKS + 1)
                nc.vector.tensor_scalar(amax_e[:].bitcast(U32), top.bitcast(U32), EXP_MASK, None,
                                        ALU.bitwise_and).then_inc(amax_e_done, 1)

            def scale_value(v):
                dve.wait_ge(amax_e_done, v + 1)
                if v >= 2:
                    dve.wait_ge(xq_done, SUB * (v - 1))
                nc.vector.tensor_scalar(scale[:, v % 2], amax_e[:], AMAX_FLOOR,
                                        2.0 ** -E4M3_EMAX, ALU.max, ALU.mult) \
                    .then_inc(scale_done, 1)

            def scale_inverse(v):
                dve.wait_ge(scale_done, v + 1)
                nc.vector.tensor_scalar(inv[:].bitcast(I32), scale[:, v % 2].bitcast(I32), -1.0,
                                        float(254 * MANTISSA), ALU.mult, ALU.add) \
                    .then_inc(inv_done, 1)

            def gated_inverse(v):
                dve.wait_ge(inv_done, v + 1)
                nc.vector.tensor_tensor(inv_g[:], inv[:],
                                        gate[:].unsqueeze(2).to_broadcast([P, SUB, NB]), ALU.mult) \
                    .then_inc(inv_g_done, 1)

            def scaled(v, t):
                src = ffn_w_f[:, SUB * v:SUB * (v + 1)] if v < WBLOCKS else x2[:, (v - WBLOCKS) % 3]
                by = inv if v < WBLOCKS else inv_g
                if v < WBLOCKS:
                    dve.wait_ge(inv_done, v + 1)
                else:
                    dve.wait_ge(inv_g_done, v - WBLOCKS + 1)
                nc.vector.tensor_tensor(
                    h[:, v % 2, t, :].rearrange("p (n k) -> p n k", k=BLOCK),
                    src[:, t, :].rearrange("p (n k) -> p n k", k=BLOCK),
                    by[:, t, :].unsqueeze(2).to_broadcast([P, NB, BLOCK]), ALU.mult) \
                    .then_inc(h_done, 1)

            def round_sum(v, t):
                dve.wait_ge(h_mag_done, SUB * v + t + 1)
                nc.vector.scalar_tensor_tensor(out=h_sum[:, t, :], in0=h_mag[:, v % 2, t, :],
                                               scalar=ROUND_FLOOR, in1=h[:, v % 2, t, :],
                                               op0=ALU.max, op1=ALU.add) \
                    .then_inc(h_sum_done, 1)

            def round_back(v, t0=0, t1=SUB):
                dve.wait_ge(h_sum_done, SUB * v + t1)
                nc.vector.scalar_tensor_tensor(out=h_round[:, t0:t1], in0=h_mag[:, v % 2, t0:t1],
                                               scalar=ROUND_FLOOR, in1=h_sum[:, t0:t1],
                                               op0=ALU.max, op1=ALU.subtract) \
                    .then_inc(h_round_done, t1 - t0)

            def clip(v, t0=0, t1=SUB):
                dve.wait_ge(h_round_done, SUB * v + t1)
                if v >= 2:
                    dve.wait_ge(xq_done, SUB * (v - 1))
                nc.vector.tensor_scalar(h_clip[:, v % 2, t0:t1], h_round[:, t0:t1], E4M3_MAX,
                                        -E4M3_MAX, ALU.min, ALU.max) \
                    .then_inc(h_clip_done, t1 - t0)

            nc.vector.memset(warm[:], 0.0).then_inc(warm_zeroed, 1)
            nc.vector.memset(mix_w[:], 0.0).then_inc(mix_w_zeroed, 1)
            lengths()
            iotas()
            split_wqkv_lo()
            block_max(0, 0)
            block_max(0, 1)
            scale_exponent(0)
            scale_value(0)
            scale_inverse(0)
            scaled(0, 0)
            scaled(0, 1)
            band_matrix()
            round_sum(0, 0)
            split_wo_lo()
            round_sum(0, 1)
            round_back(0)
            clip(0)
            block_max(1, 0)
            block_max(1, 1)
            scale_exponent(1)
            scale_value(1)
            scale_inverse(1)
            score_max(0)
            scaled(1, 0)
            scaled(1, 1)
            for s in range(UNITS - 1):
                softmax_inverse(s)
                softmax_divide(s)
                if s + 1 >= WBLOCKS:
                    gate_denominator(s + 1)
                    gate_value(s + 1)
                    gated_max(s + 1)
                softmax_turn(s, 0)
                if s + 1 >= WBLOCKS:
                    scale_exponent(s + 1)
                softmax_turn(s, 1)
                if s + 1 >= WBLOCKS:
                    scale_value(s + 1)
                softmax_turn(s, 2)
                if s + 1 >= WBLOCKS:
                    scale_inverse(s + 1)
                    gated_inverse(s + 1)
                softmax_turn(s, 3)
                if s + 1 >= WBLOCKS:
                    scaled(s + 1, 0)
                    scaled(s + 1, 1)
                round_sum(s + 1, 0)
                copy_o_lo(s)
                round_sum(s + 1, 1)
                round_back(s + 1)
                residual_sum(s, 0)
                clip(s + 1)
                masked_sum(s, 0)
                block_max(s + WBLOCKS, 0)
                residual_sum(s, 1)
                score_max(s + 1)
                masked_sum(s, 1)
                block_max(s + WBLOCKS, 1)
            softmax_inverse(UNITS - 1)
            softmax_divide(UNITS - 1)
            softmax_turn(UNITS - 1, 0)
            gate_denominator(UNITS)
            gate_value(UNITS)
            gated_max(UNITS)
            scale_exponent(UNITS)
            softmax_turn(UNITS - 1, 1)
            scale_value(UNITS)
            softmax_turn(UNITS - 1, 2)
            scale_inverse(UNITS)
            gated_inverse(UNITS)
            softmax_turn(UNITS - 1, 3)
            scaled(UNITS, 0)
            scaled(UNITS, 1)
            round_sum(UNITS, 0)
            copy_o_lo(UNITS - 1)
            round_sum(UNITS, 1)
            round_back(UNITS)
            residual_sum(UNITS - 1, 0)
            residual_sum(UNITS - 1, 1)
            masked_sum(UNITS - 1, 0)
            clip(UNITS)
            masked_sum(UNITS - 1, 1)
            block_max(STEPS - 1, 0)
            block_max(STEPS - 1, 1)
            gate_denominator(UNITS + 1)
            gate_value(UNITS + 1)
            gated_max(UNITS + 1)
            scale_exponent(UNITS + 1)
            scale_value(UNITS + 1)
            scale_inverse(UNITS + 1)
            gated_inverse(UNITS + 1)
            scaled(STEPS - 1, 0)
            scaled(STEPS - 1, 1)
            round_sum(STEPS - 1, 0)
            round_back(STEPS - 1, 0, 1)
            round_sum(STEPS - 1, 1)
            clip(STEPS - 1, 0, 1)
            round_back(STEPS - 1, 1, 2)
            clip(STEPS - 1, 1, 2)
            for u in (UNITS - 2, UNITS - 1):
                for t in range(SUB):
                    final_sum(nc.vector, u, t)


_INS = ['x', 'itok_B_0_15', 'itok_B_9_3973', 'L0_cond_weights', 'L0_attn_Wqkv', 'L0_attn_bqkv', 'L0_attn_Wo',
        'L0_attn_bo', 'L0_cond2_conv_w', 'L0_ffn_weight', 'L0_ffn_bias']
_OUTS = [((64, 32, 512), 'float32')]


def kernel(**inputs):
    import numpy as _np
    import concourse.bacc as _bacc
    from concourse import mybir as _mybir
    from concourse.bass_utils import run_bass_kernel_spmd as _run

    nc = _bacc.Bacc("TRN2", target_bir_lowering=False, num_devices=1)
    arrays, args = {}, []
    for name in _INS:
        a = _np.ascontiguousarray(inputs[name])
        arrays[f"in_{name}_dram"] = a
        args.append(nc.dram_tensor(f"in_{name}_dram", a.shape, _mybir.dt.from_np(a.dtype), kind="ExternalInput").ap())
    for i, (shape, dtype) in enumerate(_OUTS):
        dt = _mybir.dt.from_np(_np.dtype(dtype))
        args.append(nc.dram_tensor(f"out_{i}_dram", shape, dt, kind="ExternalOutput").ap())
    adaln_attn_ffn_kernel(nc, *args)
    r = _run(nc, [arrays], core_ids=[0])
    got = tuple(r.results[0][f"out_{i}_dram"] for i in range(len(_OUTS)))
    return got[0]
```
